# Optimizing a Trainium2 kernel written in Bass

```python
import numpy as np
import jax
import jax.numpy as jnp

def _softmax(x, axis=-1):
    return jax.nn.softmax(x, axis=axis)

def _gelu(x):
    return jax.nn.gelu(x, approximate=True)

def _silu(x):
    return jax.nn.silu(x)

def _sigmoid(x):
    return jax.nn.sigmoid(x)

def _layernorm(x, axis=-1, eps=1e-05):
    m = jnp.mean(x, axis=axis, keepdims=True)
    v = jnp.var(x, axis=axis, keepdims=True)
    return (x - m) / jnp.sqrt(v + eps)

def _scatter_add(tgt, idx, src, axis=0):
    return tgt.at[idx].add(src)

def _segment_sum(src, seg, n):
    return jax.ops.segment_sum(src, seg, n)
kernel_name = 'mk_prb_d1_jaxref_r8_77c25b'

def setup_inputs(seed: int=0):
    np.random.seed(seed)
    _w = jnp.asarray

    def _L0_attn_setup():
        import math
        import jax, jax.numpy as jnp
        import numpy as np
        B, L, D, H, DK = (4, 128, 128, 16, 64)
        key = jax.random.key(seed)
        ks = jax.random.split(key, 9)
        s = 0.02
        return {'source': jax.random.normal(ks[0], (B, L, D), dtype=jnp.float32), 'Wq': jax.random.normal(ks[1], (H, D, DK), dtype=jnp.float32) * s, 'bq': jax.random.normal(ks[2], (H, DK), dtype=jnp.float32) * s, 'Wk': jax.random.normal(ks[3], (H, D, DK), dtype=jnp.float32) * s, 'bk': jax.random.normal(ks[4], (H, DK), dtype=jnp.float32) * s, 'Wv': jax.random.normal(ks[5], (H, D, DK), dtype=jnp.float32) * s, 'bv': jax.random.normal(ks[6], (H, DK), dtype=jnp.float32) * s, 'Wc': jax.random.normal(ks[7], (H * DK, D), dtype=jnp.float32) * s, 'bc': jax.random.normal(ks[8], (D,), dtype=jnp.float32) * s}
    _L0_attn_in = _L0_attn_setup()

    def _L0_ffn_setup():
        import jax, jax.numpy as jnp
        import numpy as np
        E = 8
        TOP_K = 2
        ROUTE_SCALE = 1.0
        ALPHA = 1.702
        LIMIT = 7.0
        D = 128
        F = 128
        B, S = (2, 128)

        def swiglu(h):
            g = jnp.minimum(h[..., ::2], LIMIT)
            l = jnp.clip(h[..., 1::2], -LIMIT, LIMIT)
            return g * jax.nn.sigmoid(ALPHA * g) * (l + 1.0)
        if __name__ == '__main__':
            out = reference(**setup_inputs())
            print(out.shape, out.dtype)
        key = jax.random.key(seed)
        ks = jax.random.split(key, 16)
        sd = 1.0 / np.sqrt(D)
        sf = 1.0 / np.sqrt(F)
        return {'x': jax.random.normal(ks[0], (B, S, D), jnp.float32), 'gate_w': jax.random.normal(ks[1], (E, D), jnp.float32) * sd, 'gate_b': jax.random.normal(ks[2], (E,), jnp.float32) * 0.01, 'w1': jax.random.normal(ks[3], (E, 2 * F, D), jnp.float32) * sd, 'b1': jax.random.normal(ks[4], (E, 2 * F), jnp.float32) * 0.01, 'w3': jax.random.normal(ks[5], (E, 2 * F, D), jnp.float32) * sd, 'b3': jax.random.normal(ks[6], (E, 2 * F), jnp.float32) * 0.01, 'w2': jax.random.normal(ks[7], (E, D, F), jnp.float32) * sf, 'b2': jax.random.normal(ks[8], (E, D), jnp.float32) * 0.01, 'sw1': jax.random.normal(ks[9], (2 * F, D), jnp.float32) * sd, 'sb1': jax.random.normal(ks[10], (2 * F,), jnp.float32) * 0.01, 'sw3': jax.random.normal(ks[11], (2 * F, D), jnp.float32) * sd, 'sb3': jax.random.normal(ks[12], (2 * F,), jnp.float32) * 0.01, 'sw2': jax.random.normal(ks[13], (D, F), jnp.float32) * sf, 'sb2': jax.random.normal(ks[14], (D,), jnp.float32) * 0.01}
    _L0_ffn_in = _L0_ffn_setup()
    _d = {'L0_attn_source': _L0_attn_in['source'], 'L0_attn_Wq': _L0_attn_in['Wq'], 'L0_attn_bq': _L0_attn_in['bq'], 'L0_attn_Wk': _L0_attn_in['Wk'], 'L0_attn_bk': _L0_attn_in['bk'], 'L0_attn_Wv': _L0_attn_in['Wv'], 'L0_attn_bv': _L0_attn_in['bv'], 'L0_attn_Wc': _L0_attn_in['Wc'], 'L0_attn_bc': _L0_attn_in['bc'], 'L0_ffn_gate_w': _L0_ffn_in['gate_w'], 'L0_ffn_gate_b': _L0_ffn_in['gate_b'], 'L0_ffn_w1': _L0_ffn_in['w1'], 'L0_ffn_b1': _L0_ffn_in['b1'], 'L0_ffn_w3': _L0_ffn_in['w3'], 'L0_ffn_b3': _L0_ffn_in['b3'], 'L0_ffn_w2': _L0_ffn_in['w2'], 'L0_ffn_b2': _L0_ffn_in['b2'], 'L0_ffn_sw1': _L0_ffn_in['sw1'], 'L0_ffn_sb1': _L0_ffn_in['sb1'], 'L0_ffn_sw3': _L0_ffn_in['sw3'], 'L0_ffn_sb3': _L0_ffn_in['sb3'], 'L0_ffn_sw2': _L0_ffn_in['sw2'], 'L0_ffn_sb2': _L0_ffn_in['sb2']}
    _x0 = _d['L0_attn_source']
    _d['L0_attn_source'] = jax.random.normal(jax.random.fold_in(jax.random.key(seed), 1), (32, 256, 128), dtype=_x0.dtype)
    del _x0
    return _d

def reference(L0_attn_source, L0_attn_Wq, L0_attn_bq, L0_attn_Wk, L0_attn_bk, L0_attn_Wv, L0_attn_bv, L0_attn_Wc, L0_attn_bc, L0_ffn_gate_w, L0_ffn_gate_b, L0_ffn_w1, L0_ffn_b1, L0_ffn_w3, L0_ffn_b3, L0_ffn_w2, L0_ffn_b2, L0_ffn_sw1, L0_ffn_sb1, L0_ffn_sw3, L0_ffn_sb3, L0_ffn_sw2, L0_ffn_sb2):

    def _L0_attn_ref(source, Wq, bq, Wk, bk, Wv, bv, Wc, bc):
        import math
        import jax, jax.numpy as jnp
        import numpy as np
        B, L, D, H, DK = (4, 128, 128, 16, 64)
        Ln = source.shape[1]
        dk = Wq.shape[-1]
        q = jnp.einsum('bld,hdk->bhlk', source, Wq) + bq[None, :, None, :]
        k = jnp.einsum('bld,hdk->bhlk', source, Wk) + bk[None, :, None, :]
        v = jnp.einsum('bld,hdk->bhlk', source, Wv) + bv[None, :, None, :]
        scores = jnp.einsum('bhqd,bhkd->bhqk', q, k) / math.sqrt(dk)
        mask = jnp.triu(jnp.full((Ln, Ln), -jnp.inf, dtype=scores.dtype), k=1)
        attn = jax.nn.softmax(scores + mask, axis=2)
        out = jnp.einsum('bhqk,bhkd->bhqd', attn, v)
        heads = out.transpose(0, 2, 1, 3).reshape(out.shape[0], Ln, -1)
        return heads @ Wc + bc

    def _L0_ffn_ref(x, gate_w, gate_b, w1, b1, w3, b3, w2, b2, sw1, sb1, sw3, sb3, sw2, sb2):
        import jax, jax.numpy as jnp
        import numpy as np
        E = 8
        TOP_K = 2
        ROUTE_SCALE = 1.0
        ALPHA = 1.702
        LIMIT = 7.0
        D = 128
        F = 128
        B, S = (2, 128)

        def swiglu(h):
            g = jnp.minimum(h[..., ::2], LIMIT)
            l = jnp.clip(h[..., 1::2], -LIMIT, LIMIT)
            return g * jax.nn.sigmoid(ALPHA * g) * (l + 1.0)
        if __name__ == '__main__':
            out = reference(**setup_inputs())
            print(out.shape, out.dtype)
        inp_shape = x.shape
        xt = x.reshape(-1, D)
        logits = xt @ gate_w.T
        scores = jax.nn.softmax(logits.astype(jnp.float32), axis=-1)
        biased = scores + gate_b.astype(jnp.float32)
        idx = jax.lax.top_k(biased, TOP_K)[1]
        weights = (jnp.take_along_axis(scores, idx, axis=-1) * ROUTE_SCALE).astype(x.dtype)
        cw = jnp.sum(jax.nn.one_hot(idx, E, dtype=x.dtype) * weights[..., None], axis=1)
        h1 = jnp.einsum('td,efd->etf', xt, w1) + b1[:, None, :]
        h3 = jnp.einsum('td,efd->etf', xt, w3) + b3[:, None, :]
        a = swiglu(h1 * h3)
        y = jnp.einsum('etf,edf->etd', a, w2) + b2[:, None, :]
        routed = jnp.einsum('te,etd->td', cw, y)
        sh = swiglu((xt @ sw1.T + sb1) * (xt @ sw3.T + sb3))
        shared = sh @ sw2.T + sb2
        return (routed + shared).reshape(inp_shape)
    x = L0_attn_source
    xn = _layernorm(x, axis=-1)
    x = x + _L0_attn_ref(xn, L0_attn_Wq, L0_attn_bq, L0_attn_Wk, L0_attn_bk, L0_attn_Wv, L0_attn_bv, L0_attn_Wc, L0_attn_bc) + _L0_ffn_ref(xn, L0_ffn_gate_w, L0_ffn_gate_b, L0_ffn_w1, L0_ffn_b1, L0_ffn_w3, L0_ffn_b3, L0_ffn_w2, L0_ffn_b2, L0_ffn_sw1, L0_ffn_sb1, L0_ffn_sw3, L0_ffn_sb3, L0_ffn_sw2, L0_ffn_sb2)
    return x

_drawn_inputs = setup_inputs


def setup_inputs(seed=0):
    import zlib

    import numpy as np

    out = dict(_drawn_inputs(seed))
    spreads = {}
    factors = {'L0_attn_Wq': 8.0,
     'L0_attn_bq': 64.0,
     'L0_attn_Wk': 8.0,
     'L0_attn_bk': 8.0,
     'L0_attn_Wv': 3.716,
     'L0_attn_bv': 4.507,
     'L0_attn_Wc': 2.904,
     'L0_attn_bc': 3.936,
     'L0_ffn_b1': 8.0,
     'L0_ffn_b3': 8.0,
     'L0_ffn_b2': 23.99,
     'L0_ffn_sb1': 6.761,
     'L0_ffn_sb3': 7.356,
     'L0_ffn_sb2': 8.0}
    for name, (base, spread) in spreads.items():
        noise = np.random.default_rng([zlib.crc32(name.encode()), seed]).standard_normal(out[name].shape)
        drawn = base * np.exp(spread * noise) if base else spread * noise
        out[name] = jnp.asarray(drawn.astype(out[name].dtype))
    for name, factor in factors.items():
        out[name] = (out[name] * factor).astype(out[name].dtype)
    return out
```

```python
from contextlib import ExitStack

import concourse.bass as bass
from concourse import mybir

ALU = mybir.AluOpType
ACT = mybir.ActivationFunctionType
AX = mybir.AxisListType
F32 = mybir.dt.float32
F32R = mybir.dt.float32r

P = 128
H, DK = 16, 64
PAIRS = H // 2
E = 8
LIMIT = 7.0
ALPHA = 1.702
EPS = 1e-5
MASKED = -1e30
GROUP = 4


def causal_cols(kt, L):
    return L - P * kt


def build(nc, source, Wq, bq, Wk, bk, Wv, bv, Wc, bc, gate_w, gate_b, w1, b1, w3, b3, w2, b2,
          sw1, sb1, sw3, sb3, sw2, sb2, out):
    B, L, D = source.shape
    assert D == P and L == 2 * P
    KT = L // P
    TILES = B * KT
    GROUPS = TILES // GROUP
    NE = E + 1
    SCALE = float(DK) ** -0.5
    QCOLS = [causal_cols(kt, L) for kt in range(KT)]
    QOFF = [sum(QCOLS[:kt]) for kt in range(KT)]
    SW = sum(QCOLS)
    SMALL = 17
    ROUTED = 19

    x_rows = source.rearrange("b l d -> (b l) d")
    out_rows = out.rearrange("b l d -> (b l) d")
    xnT_dram = nc.dram_tensor("xnT_dram", (B, P, 2 * L), F32).ap()

    ctx = ExitStack()
    with ctx:
        def sb(name, shape, dt=F32):
            return ctx.enter_context(nc.sbuf_tensor(name, shape, dt))

        def ps(name):
            return ctx.enter_context(nc.psum_tensor(name, [P, 512], F32))

        def sem(name):
            return ctx.enter_context(nc.semaphore(name))

        ident = sb("ident", [P, P])
        mask = sb("mask", [P, L])
        ones2 = sb("ones2", [P, P], F32R)
        wqkv = [sb(f"wqkv{part}", [P, 3, H * DK], F32R) for part in range(2)]
        w13 = [sb(f"w13{part}", [P, NE, 4 * P], F32R) for part in range(2)]
        w2T = sb("w2T", [P, NE, P])
        wc = sb("wc", [P, PAIRS, P])
        gateT = [sb(f"gateT{part}", [P, E], F32R) for part in range(2)]
        b13 = sb("b13", [P, NE, 4 * P], F32R)
        bvr = sb("bvr", [P, H * DK], F32R)
        bqk = sb("bqk", [P, 2, PAIRS])
        gate_bb = sb("gate_bb", [P, E])
        out_bias = sb("out_bias", [P, 3, P])
        b2_bb = sb("b2_bb", [P, E, P])
        bias_raw = sb("bias_raw", [P, NE, 2, 2 * P])
        bv_raw = sb("bv_raw", [P, H * DK])
        raw = sb("raw", [P, 4, 1024])
        xg = sb("xg", [P, 2, GROUP, P])
        stats = sb("stats", [P, 2, GROUP, 6])
        moments = sb("moments", [P, 2, GROUP, 2])
        rstd = sb("rstd", [P, 2, GROUP])
        xnT = [sb(f"xnT{part}", [P, 2, GROUP * P], F32R) for part in range(2)]
        logits = sb("logits", [P, TILES, E])
        gtmp = [sb(f"gtmp{i}", [P, TILES, E]) for i in range(3)]
        gred = sb("gred", [P, TILES])
        gred2 = sb("gred2", [P, TILES])
        rank_key = sb("rank_key", [P, E])
        combine = sb("combine", [P, TILES, NE])
        half_cw = sb("half_cw", [P, 2, KT, NE])
        xT = [sb(f"xT{par}", [P, 2, L], F32R) for par in range(2)]
        xres = [sb(f"xres{par}", [P, KT, P]) for par in range(2)]
        yout = [sb(f"yout{par}", [P, KT, P]) for par in range(2)]
        qk = sb("qk", [P, 2, 2, L])
        masked_s = sb("masked_s", [P, 2, 2, SW])
        probs = sb("probs", [P, 2, 2, SW])
        neg_max = sb("neg_max", [P, 2, 2, KT])
        denom = sb("denom", [P, 2, KT, 2])
        rdenom = sb("rdenom", [P, 2, KT, 2])
        vs = sb("vs", [P, 2, KT, P])
        headsT = sb("headsT", [P, 2, L])
        h1 = sb("h1", [P, 2, 2 * P])
        hgl = sb("hgl", [P, 2, 2 * P])
        gmin = sb("gmin", [P, 2, P])
        lclip = sb("lclip", [P, 2, P])
        lscaled = sb("lscaled", [P, 2, P])
        th = sb("th", [P, 2, P])
        tg = sb("tg", [P, 2, P])
        act_a = sb("act_a", [P, 2, P])
        aT = sb("aT", [P, 2, P])

        p_qk, p_v, p_s0, p_s1, p_o, p_acc, p_h, p_t = [ps(n) for n in
            ("p_qk", "p_v", "p_s0", "p_s1", "p_o", "p_acc", "p_h", "p_t")]
        p_s = [p_s0, p_s1]
        logit_ps = p_v[:, :].rearrange("p (t e) -> p t e", e=E)

        zeroed = sem("zeroed")
        consts = sem("consts")
        raw_qkv_in = sem("raw_qkv_in")
        raw_13_in = [sem(f"raw_13_in{i}") for i in range(2)]
        raw_w2_in = sem("raw_w2_in")
        small_in = sem("small_in")
        wT_done = sem("wT_done")
        wT_evac_hi = sem("wT_evac_hi")
        wT_evac = sem("wT_evac")
        qkv_hi = sem("qkv_hi")
        weights_ready = sem("weights_ready")
        dve_step = sem("dve_step")
        xg_in = [sem(f"xg_in{i}") for i in range(2)]
        stats_done = sem("stats_done")
        moments_done = sem("moments_done")
        var_done = sem("var_done")
        std_done = sem("std_done")
        rstd_done = sem("rstd_done")
        xn_done = sem("xn_done")
        xnT_done = sem("xnT_done")
        xnT_hi = sem("xnT_hi")
        xnT_lo = sem("xnT_lo")
        xnT_stored = [sem(f"xnT_stored{i}") for i in range(2)]
        logits_done = sem("logits_done")
        gate_exp = sem("gate_exp")
        gate_sub = sem("gate_sub")
        routed = sem("routed")
        xT_in = [sem(f"xT_in{i}") for i in range(2)]
        xres_in = [sem(f"xres_in{i}") for i in range(2)]
        resid_done = sem("resid_done")
        out_stored = [sem(f"out_stored{i}") for i in range(2)]
        y_ready = sem("y_ready")
        qk_proj = sem("qk_proj")
        qk_ready = sem("qk_ready")
        scores_done = sem("scores_done")
        masked = sem("masked")
        probs_ready = sem("probs_ready")
        rdenom_done = sem("rdenom_done")
        v_proj = sem("v_proj")
        v_scaled = sem("v_scaled")
        av_done = sem("av_done")
        heads_ready = sem("heads_ready")
        wc_done = sem("wc_done")
        h_done = sem("h_done")
        h1_copied = sem("h1_copied")
        hgl_done = sem("hgl_done")
        g_ready = sem("g_ready")
        l_ready = sem("l_ready")
        l_scaled = sem("l_scaled")
        tanh_done = sem("tanh_done")
        tg_done = sem("tg_done")
        a_ready = sem("a_ready")
        aT_done = sem("aT_done")
        aT_ready = sem("aT_ready")
        y_done = sem("y_done")
        cw_ready = sem("cw_ready")
        b2_step = sem("b2_step")
        waits_apart = sem("waits_apart")

        def apart(eng):
            eng.sem_inc(waits_apart, 1)

        block = ctx.enter_context(nc.Block())

        def w13_raw(e):
            return raw[:, 2 + e % 2, 0:4 * P].rearrange("p (w u d) -> p w u d", w=2, u=2)

        def w2_raw():
            return raw[:, 0:2, :].rearrange("p a b -> p (a b)")[:, 0:NE * P].rearrange("p (e f) -> p e f", e=NE)

        gate_raw = raw[0:E, 1, 896:1024]
        UNITS = [(tt, e) for tt in range(KT) for e in range(NE)]
        STEPS = PAIRS + 2
        NU = len(UNITS)

        def units_of(step):
            return range(min(2 * step, NU), min(2 * step + 2, NU))

        @block.sync
        def _(sp):
            for i, w in enumerate((Wq, Wk, Wv)):
                sp.dma_start(raw[:, i, :].rearrange("p (h k) -> p h k", h=H),
                             w.rearrange("h d k -> d h k")).then_inc(raw_qkv_in, 16)
            small = [
                (wc[:, :, :], Wc.rearrange("(c p) n -> p c n", p=P)),
                (bqk[:, 0, :], bq.rearrange("(c u) k -> (u k) c", u=2)),
                (bqk[:, 1, :], bk.rearrange("(c u) k -> (u k) c", u=2)),
                (gate_bb[:, :], gate_b.rearrange("(a e) -> a e", a=1).to_broadcast([P, E])),
                (out_bias[:, 0, :], bc.rearrange("(a e) -> a e", a=1).to_broadcast([P, P])),
                (out_bias[:, 1, :], sb2.rearrange("(a e) -> a e", a=1).to_broadcast([P, P])),
                (b2_bb[:, :, :].rearrange("p e d -> p (e d)"),
                 b2.rearrange("(a e) d -> a (e d)", a=1).to_broadcast([P, E * P])),
            ]
            for row in (0, 32):
                small += [
                    (bv_raw[row:row + 1, :], bv.rearrange("(a h) k -> a (h k)", a=1)),
                    (bias_raw[row:row + 1, 0:E, 0, :], b1.rearrange("(a e) f -> a e f", a=1)),
                    (bias_raw[row:row + 1, 0:E, 1, :], b3.rearrange("(a e) f -> a e f", a=1)),
                    (bias_raw[row:row + 1, E, 0, :], sb1.rearrange("(a f) -> a f", a=1)),
                    (bias_raw[row:row + 1, E, 1, :], sb3.rearrange("(a f) -> a f", a=1)),
                ]
            bqk_t = bqk[:, 0, :].tensor
            for dst, src in small:
                sp.dma_start(dst, src, allow_slow_non_contiguous=dst.tensor is bqk_t).then_inc(small_in, 16)
            assert len(small) == SMALL
            for e in range(NE):
                if e == 0:
                    sp.wait_ge(weights_ready, 1)
                if e >= 2:
                    sp.wait_ge(wT_done, e - 1)
                for i, w in enumerate((w1[e], w3[e]) if e < E else (sw1, sw3)):
                    sp.dma_start(w13_raw(e)[:, i], w.rearrange("(u p) d -> p u d", p=P)).then_inc(raw_13_in[e % 2], 16)
            sp.wait_ge(weights_ready, 1)
            sp.dma_start(w2_raw()[:, 0:E, :], w2.rearrange("e d f -> d e f")).then_inc(raw_w2_in, 16)
            sp.dma_start(w2_raw()[:, E, :], sw2).then_inc(raw_w2_in, 16)
            sp.dma_start(gate_raw, gate_w).then_inc(raw_w2_in, 16)

            def load_x(g, par):
                sp.dma_start(xg[:, par], x_rows[bass.ds(g * GROUP * P, GROUP * P)]
                             .rearrange("(t p) d -> p t d", p=P)).then_inc(xg_in[par], 16)

            def store_xnT(g, par):
                sp.wait_ge(xnT_lo, g + 1)
                apart(sp)
                for part in range(2):
                    dst = xnT_dram[bass.ds(g * (GROUP // KT), GROUP // KT)].rearrange("s p (a l) -> p s a l", a=2)[:, :, part]
                    sp.dma_start(dst, xnT[part][:, par].bitcast(F32).rearrange("p (s l) -> p s l", l=L)).then_inc(xnT_stored[par], 16)

            load_x(0, 0)
            load_x(1, 1)
            with sp.Fori(0, GROUPS // 2 - 1) as i:
                for par in range(2):
                    sp.wait_ge(xnT_done, 2 * i + par + 1)
                    apart(sp)
                    load_x(2 * i + par + 2, par)
                    store_xnT(2 * i + par, par)
            store_xnT(GROUPS - 2, 0)
            store_xnT(GROUPS - 1, 1)

            for par in range(2):
                sp.wait_ge(xnT_stored[par], 16 * GROUPS)

            def load_seq(i, par):
                b = 2 * i + par
                sp.dma_start(xT[par][:, :, :].bitcast(F32).rearrange("p a l -> p (a l)"), xnT_dram[bass.ds(b, 1)].rearrange("s p n -> (s p) n")).then_inc(xT_in[par], 16)
                sp.dma_start(xres[par][:, :, :], x_rows[bass.ds(b * L, L)].rearrange("(t p) d -> p t d", p=P)).then_inc(xres_in[par], 16)

            def store_seq(i, par):
                b = 2 * i + par
                sp.wait_ge(y_ready, b + 1)
                apart(sp)
                sp.dma_start(out_rows[bass.ds(b * L, L)].rearrange("(t p) d -> p t d", p=P),
                             yout[par][:, :, :]).then_inc(out_stored[par], 16)

            load_seq(0, 0)
            load_seq(0, 1)
            with sp.Fori(1, B // 2) as i:
                for par in range(2):
                    sp.wait_ge(y_ready, 2 * i + par - 1)
                    apart(sp)
                    sp.wait_ge(wc_done, PAIRS * (2 * i + par - 1))
                    apart(sp)
                    load_seq(i, par)
                    store_seq(i - 1, par)
            for par in range(2):
                store_seq(B // 2 - 1, par)
            for par in range(2):
                sp.wait_ge(out_stored[par], 16 * (B // 2))

        @block.gpsimd
        def _(pool):
            pool.memset(ident[:, :], 0.0).then_inc(zeroed, 1)
            pool.memset(mask[:, :], 0.0).then_inc(zeroed, 1)
            pool.memset(ones2[:, :].bitcast(F32), 0.0).then_inc(zeroed, 1)
            pool.memset(b13[:, :, :].bitcast(F32), 0.0).then_inc(zeroed, 1)
            pool.memset(bvr[:, :].bitcast(F32), 0.0).then_inc(zeroed, 1)
            for e in range(E):
                pool.memset(rank_key[:, e:e + 1], float(E - e)).then_inc(zeroed, 1)
            pool.memset(combine[:, :, :].rearrange("p t e -> p (t e)"), 1.0).then_inc(zeroed, 1)
            pool.wait_ge(zeroed, 6 + E)
            pool.affine_select(out=ident[:, :], in_=ident[:, :], compare_op=ALU.not_equal, fill=1.0, base=0,
                               pattern=[[-1, P]], channel_multiplier=1).then_inc(consts, 1)
            pool.affine_select(out=mask[:, 0:P], in_=mask[:, 0:P], compare_op=ALU.is_ge, fill=MASKED, base=0,
                               pattern=[[1, P]], channel_multiplier=-1).then_inc(consts, 1)
            for n, row in enumerate((0, 32)):
                pool.wait_ge(consts, 2 + n)
                pool.memset(ones2[row:row + 1, :].bitcast(F32), 1.0).then_inc(consts, 1)

            def residual(i, par):
                b = 2 * i + par
                pool.wait_ge(xres_in[par], 16 * (i + 1))
                pool.tensor_tensor(xres[par][:, :, :], xres[par][:, :, :],
                                   out_bias[:, 2, :].unsqueeze(1).to_broadcast([P, KT, P]), ALU.add).then_inc(resid_done, 1)

            def weights_of_seq(i, par):
                b = 2 * i + par
                if not (isinstance(i, int) and i == 0):
                    pool.wait_ge(y_ready, b - 1)
                pool.tensor_copy(half_cw[:, par, :, :], combine[:, bass.ds(b * KT, KT), :]).then_inc(cw_ready, 1)

            pool.wait_ge(weights_ready, 2)
            pool.wait_ge(routed, ROUTED)
            for par in range(2):
                weights_of_seq(0, par)
                residual(0, par)
            with pool.Fori(1, B // 2) as i:
                for par in range(2):
                    weights_of_seq(i, par)
                    residual(i, par)

        @block.scalar
        def _(act):
            act.wait_ge(raw_qkv_in, 48)
            for i in range(3):
                act.activation(wqkv[0][:, i, :], raw[:, i, :], ACT.Copy).then_inc(qkv_hi, 1)
            for e in range(NE):
                act.wait_ge(wT_done, e + 1)
                for w in range(2):
                    act.activation(w13[0][:, e, 2 * P * w:2 * P * (w + 1)].rearrange("p (two j) -> p two j", two=2),
                                   p_s[e % 2][:, 2 * P * w:2 * P * (w + 1)].rearrange("p (j two) -> p two j", two=2),
                                   ACT.Copy).then_inc(wT_evac_hi, 1)
            for k, bank in enumerate((p_o, p_h, p_t)):
                n = min(4, NE - 4 * k)
                act.wait_ge(wT_done, NE + k + 1)
                act.activation(w2T[:, 4 * k:4 * k + n, :].rearrange("p e d -> p (e d)"), bank[:, 0:n * P],
                               ACT.Copy, scale=0.5).then_inc(weights_ready, 1)
            act.activation(gateT[0][:, :], p_t[:, P:P + E], ACT.Copy).then_inc(wT_evac_hi, 1)

            def first_pass(g, par, first=False):
                act.wait_ge(var_done, g + 1)
                act.activation(rstd[:, par, :], rstd[:, par, :], ACT.Sqrt).then_inc(std_done, 1)
                act.wait_ge(xnT_done, g + 1)
                if not first:
                    act.wait_ge(xnT_stored[par], 16 * (g - par))
                act.activation(xnT[0][:, par, :], p_s[par][:, :], ACT.Copy).then_inc(xnT_hi, 1)

            for par in range(2):
                first_pass(par, par, first=True)
            with act.Fori(1, GROUPS // 2) as i:
                for par in range(2):
                    first_pass(2 * i + par, par)
            act.wait_ge(gate_sub, 2)
            act.activation(gtmp[0][:, :, :], gtmp[0][:, :, :], ACT.Exp).then_inc(gate_exp, 1)

            def qk_evac(b, p):
                act.wait_ge(qk_proj, PAIRS * b + p + 1)
                for j in range(2):
                    ins = act.activation(qk[:, p % 2, j, :], p_qk[:, j * L:(j + 1) * L], ACT.Identity,
                                         bias=bqk[:, j, p:p + 1])
                ins.then_inc(qk_ready, 1)

            def exps(b, p, first):
                if not (first and p < 2):
                    act.wait_ge(av_done, PAIRS * b + p - 1)
                    act.wait_ge(rdenom_done, PAIRS * b + p - 1)
                for hh in range(2):
                    act.wait_ge(masked, 2 * (PAIRS * b + p) + hh + 1)
                    for kt in range(KT):
                        cols = slice(QOFF[kt], QOFF[kt] + QCOLS[kt])
                        ins = act.activation(probs[:, p % 2, hh, cols], masked_s[:, p % 2, hh, cols], ACT.Exp,
                                             bias=neg_max[:, p % 2, hh, kt:kt + 1], scale=-1.0,
                                             accum_out=denom[:, p % 2, kt, hh:hh + 1])
                ins.then_inc(probs_ready, 1)

            def heads_evac(b, p, first):
                act.wait_ge(av_done, PAIRS * b + p + 1)
                if not (first and p < 2):
                    act.wait_ge(wc_done, PAIRS * b + p - 1)
                act.activation(headsT[:, p % 2, :], p_o[:, 0:L], ACT.Copy).then_inc(heads_ready, 1)

            def copy_h1(b, u, first):
                act.wait_ge(h_done, NU * b + u + 1)
                if not (first and u < 2):
                    act.wait_ge(hgl_done, NU * b + u - 1)
                act.activation(h1[:, u % 2, :], p_h[:, 0:2 * P], ACT.Copy).then_inc(h1_copied, 1)

            def tanh(b, u, first):
                act.wait_ge(g_ready, NU * b + u + 1)
                if not (first and u < 2):
                    act.wait_ge(tg_done, NU * b + u - 1)
                act.activation(th[:, u % 2, :], gmin[:, u % 2, :], ACT.Tanh, scale=ALPHA / 2).then_inc(tanh_done, 1)

            def evac_aT(b, u, first):
                act.wait_ge(aT_done, NU * b + u + 1)
                if not (first and u < 2):
                    act.wait_ge(y_done, NU * b + u - 1)
                act.activation(aT[:, u % 2, :], p_t[:, 0:P], ACT.Copy).then_inc(aT_ready, 1)

            def sequence(i, par, first):
                b = 2 * i + par
                qk_evac(b, 0)
                for s in range(STEPS):
                    if s < PAIRS:
                        exps(b, s, first)
                    for u in units_of(s):
                        copy_h1(b, u, first)
                        tanh(b, u, first)
                        evac_aT(b, u, first)
                    if s + 1 < PAIRS:
                        qk_evac(b, s + 1)
                    if 1 <= s <= PAIRS:
                        heads_evac(b, s - 1, first)

            for par in range(2):
                sequence(0, par, par == 0)
            with act.Fori(1, B // 2) as i:
                for par in range(2):
                    sequence(i, par, False)

        @block.tensor
        def _(pe):
            def three(dst, stat, mov, start, stop, **kw):
                pe.matmul(dst, stat[0], mov[0], start=start, stop=False, **kw)
                pe.matmul(dst, stat[1], mov[0], start=False, stop=False, **kw)
                return pe.matmul(dst, stat[0], mov[1], start=False, stop=stop, **kw)

            pe.wait_ge(consts, 4)
            for e in range(NE):
                pe.wait_ge(raw_13_in[e % 2], 32 * (e // 2 + 1))
                if e >= 2:
                    pe.wait_ge(wT_evac, e - 1)
                for w in range(2):
                    for u in range(2):
                        ins = pe.transpose(p_s[e % 2][:, (2 * w + u) * P:(2 * w + u + 1) * P], w13_raw(e)[:, w, u, :], ident[:, :])
                ins.then_inc(wT_done, 1)
            pe.wait_ge(raw_w2_in, 48)
            for k, bank in enumerate((p_o, p_h, p_t)):
                for e in range(4 * k, min(4 * k + 4, NE)):
                    ins = pe.transpose(bank[:, (e % 4) * P:(e % 4 + 1) * P], w2_raw()[:, e, :], ident[:, :])
                if k == 2:
                    ins = pe.transpose(p_t[:, P:P + E], gate_raw, ident[0:E, 0:E])
                ins.then_inc(wT_done, 1)

            def transposes(g, par, first=False):
                pe.wait_ge(xn_done, g + 1)
                if not first:
                    pe.wait_ge(xnT_lo, g - 1)
                for t in range(GROUP):
                    ins = pe.transpose(p_s[par][:, t * P:(t + 1) * P], xg[:, par, t, :], ident[:, :])
                ins.then_inc(xnT_done, 1)

            def gate(g, par):
                pe.wait_ge(xnT_lo, g + 1)
                for t in range(GROUP):
                    cols = slice(t * P, (t + 1) * P)
                    ins = three(logit_ps[:, bass.ds(g * GROUP + t, 1), :].rearrange("p a e -> p (a e)"),
                                [xnT[k][:, par, cols] for k in range(2)], [gateT[k][:, :] for k in range(2)],
                                start=True, stop=True, skip_group_check=True)
                ins.then_inc(logits_done, 1)

            pe.wait_ge(weights_ready, 6)
            transposes(0, 0, first=True)
            transposes(1, 1, first=True)
            gate(0, 0)
            with pe.Fori(1, GROUPS // 2) as i:
                transposes(2 * i, 0)
                gate(2 * i - 1, 1)
                transposes(2 * i + 1, 1)
                gate(2 * i, 0)
            gate(GROUPS - 1, 1)

            def project_qk(b, i, p, par):
                if p == 0:
                    pe.wait_ge(xT_in[par], 16 * (i + 1))
                if not (isinstance(b, int) and b == 0 and p == 0):
                    pe.wait_ge(qk_ready, PAIRS * b + p)
                for j in range(2):
                    ins = three(p_qk[:, j * L:(j + 1) * L], [w[:, j, p * P:(p + 1) * P] for w in wqkv],
                                [xT[par][:, k, :] for k in range(2)], start=True, stop=True)
                ins.then_inc(qk_proj, 1)

            def scores(b, p, first):
                pe.wait_ge(qk_ready, PAIRS * b + p + 1)
                for hh in range(2):
                    if not (first and p == 0):
                        pe.wait_ge(masked, 2 * (PAIRS * b + p) + hh - 1)
                    rows = slice(DK * hh, DK * (hh + 1))
                    for kt in range(KT):
                        ins = pe.matmul(p_s[hh][:, QOFF[kt]:QOFF[kt] + QCOLS[kt]],
                                        qk[rows, p % 2, 1, kt * P:(kt + 1) * P], qk[rows, p % 2, 0, kt * P:L],
                                        start=True, stop=True, skip_group_check=True)
                    ins.then_inc(scores_done, 1)

            def project_v(b, g, par):
                if not (isinstance(b, int) and b == 0 and g == 0):
                    pe.wait_ge(v_scaled, PAIRS * b + 2 * g)
                else:
                    pe.wait_ge(gate_sub, 1)
                cols = slice(g * 2 * P, (g + 1) * 2 * P)
                for kt in range(KT):
                    dst = p_v[:, kt * 2 * P:(kt + 1) * 2 * P]
                    three(dst, [xT[par][:, k, kt * P:(kt + 1) * P] for k in range(2)],
                          [w[:, 2, cols] for w in wqkv], start=True, stop=False)
                    ins = pe.matmul(dst, ones2[:, :], bvr[:, cols], start=False, stop=True)
                ins.then_inc(v_proj, 1)

            def values(b, p):
                pe.wait_ge(v_scaled, PAIRS * b + p + 1)
                if not (isinstance(b, int) and b == 0 and p == 0):
                    pe.wait_ge(heads_ready, PAIRS * b + p)
                for kt in range(KT):
                    for hh in range(2):
                        rows = slice(DK * hh, DK * (hh + 1))
                        ins = pe.matmul(p_o[rows, kt * P:L], vs[:, p % 2, kt, rows],
                                        probs[:, p % 2, hh, QOFF[kt]:QOFF[kt] + QCOLS[kt]],
                                        start=(kt == 0), stop=(kt == KT - 1), skip_group_check=True)
                ins.then_inc(av_done, 1)

            def out_projection(b, p, last):
                pe.wait_ge(heads_ready, PAIRS * b + p + 1)
                for tt in range(KT):
                    ins = pe.matmul(p_acc[:, tt * P:(tt + 1) * P], headsT[:, p % 2, tt * P:(tt + 1) * P], wc[:, p, :],
                                    start=False, stop=last and tt == KT - 1, skip_group_check=True)
                ins.then_inc(wc_done, 1)

            def expert_in(b, u, par):
                tt, e = UNITS[u]
                if not (isinstance(b, int) and b == 0 and u == 0):
                    pe.wait_ge(hgl_done, NU * b + u)
                three(p_h[:, :], [xT[par][:, k, tt * P:(tt + 1) * P] for k in range(2)],
                      [w[:, e, :] for w in w13], start=True, stop=False)
                pe.matmul(p_h[:, :], ones2[:, :], b13[:, e, :], start=False, stop=True).then_inc(h_done, 1)

            def expert_turn(b, u):
                pe.wait_ge(a_ready, NU * b + u + 1)
                if not (isinstance(b, int) and b == 0 and u == 0):
                    pe.wait_ge(aT_ready, NU * b + u)
                pe.transpose(p_t[:, 0:P], act_a[:, u % 2, :], ident[:, :]).then_inc(aT_done, 1)

            def expert_out(b, u, first):
                tt, e = UNITS[u]
                pe.wait_ge(aT_ready, NU * b + u + 1)
                if u == 0 and not (isinstance(b, int) and b == 0):
                    pe.wait_ge(y_ready, b)
                pe.matmul(p_acc[:, tt * P:(tt + 1) * P], aT[:, u % 2, :], w2T[:, e, :], start=(u == 0), stop=False,
                          skip_group_check=True).then_inc(y_done, 1)

            def sequence(i, par, first):
                b = 2 * i + par
                project_qk(b, i, 0, par)
                for s in range(STEPS):
                    if s < PAIRS:
                        scores(b, s, first)
                        if s % 2 == 0:
                            project_v(b, s // 2, par)
                    for u in units_of(s):
                        expert_in(b, u, par)
                        expert_turn(b, u)
                        expert_out(b, u, first)
                    if s + 1 < PAIRS:
                        project_qk(b, i, s + 1, par)
                    if 1 <= s <= PAIRS:
                        values(b, s - 1)
                    if s >= 2:
                        out_projection(b, s - 2, s == STEPS - 1)

            for par in range(2):
                sequence(0, par, par == 0)
            with pe.Fori(1, B // 2) as i:
                for par in range(2):
                    sequence(i, par, False)

        @block.vector
        def _(dve):
            for i in range(3):
                dve.wait_ge(qkv_hi, i + 1)
                ins = dve.tensor_tensor(wqkv[1][:, i, :], raw[:, i, :], wqkv[0][:, i, :].bitcast(F32), ALU.subtract)
            ins.then_inc(weights_ready, 1)
            dve.wait_ge(small_in, 16 * SMALL)
            dve.wait_ge(zeroed, 6 + E)
            dve.wait_ge(consts, 4)
            n = 0
            for w in range(2):
                src = bias_raw[:, :, w, :].rearrange("p e (j two) -> p e two j", two=2)
                dst = b13[:, :, 2 * P * w:2 * P * (w + 1)].rearrange("p e (two j) -> p e two j", two=2)
                for e in range(NE):
                    for row in (0, 32):
                        dve.tensor_copy(dst[row:row + 1, e], src[row:row + 1, e]).then_inc(dve_step, 1)
                        n += 1
            for row in (0, 32):
                dve.tensor_copy(bvr[row:row + 1, :], bv_raw[row:row + 1, :]).then_inc(dve_step, 1)
                n += 1
            dve.wait_ge(dve_step, n)
            for w in range(2):
                src = bias_raw[32:33, :, w, :].rearrange("p e (j two) -> p e two j", two=2)
                dst = b13[32:33, :, 2 * P * w:2 * P * (w + 1)].rearrange("p e (two j) -> p e two j", two=2)
                for e in range(NE):
                    dve.tensor_tensor(dst[:, e], src[:, e], dst[:, e].bitcast(F32), ALU.subtract)
            dve.tensor_tensor(bvr[32:33, :], bv_raw[32:33, :], bvr[32:33, :].bitcast(F32), ALU.subtract)
            dve.tensor_tensor(out_bias[:, 2, :], out_bias[:, 0, :], out_bias[:, 1, :], ALU.add).then_inc(weights_ready, 1)
            for e in range(NE):
                dve.wait_ge(wT_evac_hi, 2 * e + 2)
                for w in range(2):
                    def halves(t):
                        return t[:, 2 * P * w:2 * P * (w + 1)].rearrange("p (two j) -> p two j", two=2)
                    ins = dve.tensor_tensor(halves(w13[1][:, e]), p_s[e % 2][:, 2 * P * w:2 * P * (w + 1)].rearrange("p (j two) -> p two j", two=2),
                                            halves(w13[0][:, e]).bitcast(F32), ALU.subtract)
                ins.then_inc(wT_evac, 1)
            dve.wait_ge(wT_evac_hi, 2 * NE + 1)
            dve.tensor_tensor(gateT[1][:, :], p_t[:, P:P + E], gateT[0][:, :].bitcast(F32), ALU.subtract).then_inc(weights_ready, 1)

            def first_pass(g, i, par, first=False):
                dve.wait_ge(xg_in[par], 16 * (i + 1))
                for t in range(GROUP):
                    ins = dve.bn_stats(stats[:, par, t, :], xg[:, par, t, :])
                ins.then_inc(stats_done, 1)
                dve.wait_ge(stats_done, g + 1)
                apart(dve)
                for t in range(GROUP):
                    ins = dve.bn_aggr(moments[:, par, t, :], stats[:, par, t, :])
                ins.then_inc(moments_done, 1)
                dve.wait_ge(moments_done, g + 1)
                dve.tensor_scalar(rstd[:, par, :], moments[:, par, :, 1], EPS, None, ALU.add).then_inc(var_done, 1)
                dve.wait_ge(std_done, g + 1)
                dve.reciprocal(rstd[:, par, :], rstd[:, par, :]).then_inc(rstd_done, 1)
                dve.wait_ge(rstd_done, g + 1)
                for t in range(GROUP):
                    ins = dve.tensor_scalar(xg[:, par, t, :], xg[:, par, t, :], moments[:, par, t, 0:1], rstd[:, par, t:t + 1],
                                            ALU.subtract, ALU.mult)
                ins.then_inc(xn_done, 1)
                dve.wait_ge(xnT_hi, g + 1)
                if not first:
                    dve.wait_ge(logits_done, g - 1)
                dve.tensor_tensor(xnT[1][:, par, :], p_s[par][:, :], xnT[0][:, par, :].bitcast(F32), ALU.subtract).then_inc(xnT_lo, 1)

            for par in range(2):
                first_pass(par, 0, par, first=True)
            with dve.Fori(1, GROUPS // 2) as i:
                for par in range(2):
                    first_pass(2 * i + par, i, par)

            k = [0]

            def then(ins):
                k[0] += 1
                ins.then_inc(routed, 1)
                dve.wait_ge(routed, k[0])

            def per_expert(t):
                return t[:, :].unsqueeze(2).to_broadcast([P, TILES, E])

            ex, biased, hit = gtmp
            dve.wait_ge(logits_done, GROUPS)
            dve.tensor_copy(logits[:, :, :], logit_ps).then_inc(gate_sub, 1)
            dve.wait_ge(gate_sub, 1)
            then(dve.tensor_reduce(gred[:, :], logits[:, :, :], AX.X, ALU.max))
            dve.tensor_tensor(ex[:, :, :], logits[:, :, :], per_expert(gred), ALU.subtract).then_inc(gate_sub, 1)
            dve.wait_ge(gate_exp, 1)
            then(dve.tensor_reduce(gred[:, :], ex[:, :, :], AX.X, ALU.add))
            then(dve.reciprocal(gred2[:, :], gred[:, :]))
            then(dve.tensor_tensor(logits[:, :, :], ex[:, :, :], per_expert(gred2), ALU.mult))
            then(dve.tensor_tensor(biased[:, :, :], logits[:, :, :], gate_bb[:, :].unsqueeze(1).to_broadcast([P, TILES, E]), ALU.add))
            keys = rank_key[:, :].unsqueeze(1).to_broadcast([P, TILES, E])
            for choice in range(2):
                then(dve.tensor_reduce(gred[:, :], biased[:, :, :], AX.X, ALU.max))
                then(dve.tensor_tensor(hit[:, :, :], biased[:, :, :], per_expert(gred), ALU.is_equal))
                then(dve.tensor_tensor(hit[:, :, :], hit[:, :, :], keys, ALU.mult))
                then(dve.tensor_reduce(gred[:, :], hit[:, :, :], AX.X, ALU.max))
                then(dve.tensor_tensor(ex[:, :, :] if choice else hit[:, :, :], keys, per_expert(gred), ALU.is_equal))
                if choice == 0:
                    then(dve.tensor_tensor(combine[:, :, 0:E], hit[:, :, :], logits[:, :, :], ALU.mult))
                    then(dve.scalar_tensor_tensor(out=biased[:, :, :], in0=hit[:, :, :], scalar=MASKED, in1=biased[:, :, :],
                                                  op0=ALU.mult, op1=ALU.add))
            then(dve.tensor_tensor(ex[:, :, :], ex[:, :, :], logits[:, :, :], ALU.mult))
            then(dve.tensor_tensor(combine[:, :, 0:E], combine[:, :, 0:E], ex[:, :, :], ALU.add))
            assert k[0] == ROUTED, k[0]

            def mask_and_max(b, p, first):
                if not (first and p < 2):
                    dve.wait_ge(probs_ready, PAIRS * b + p - 1)
                for hh in range(2):
                    dve.wait_ge(scores_done, 2 * (PAIRS * b + p) + hh + 1)
                    apart(dve)
                    for kt in range(KT):
                        cols = slice(QOFF[kt], QOFF[kt] + QCOLS[kt])
                        ins = dve.tensor_tensor_reduce(out=masked_s[:, p % 2, hh, cols], in0=p_s[hh][:, cols],
                                                       in1=mask[:, 0:QCOLS[kt]], scale=-SCALE, scalar=-MASKED,
                                                       op0=ALU.add, op1=ALU.min, accum_out=neg_max[:, p % 2, hh, kt:kt + 1])
                    ins.then_inc(masked, 1)

            def scale_values(b, p, first):
                dve.wait_ge(probs_ready, PAIRS * b + p + 1)
                dve.reciprocal(rdenom[:, p % 2], denom[:, p % 2]).then_inc(rdenom_done, 1)
                dve.wait_ge(rdenom_done, PAIRS * b + p + 1)
                dve.wait_ge(v_proj, PAIRS // 2 * b + p // 2 + 1)
                if not (first and p < 2):
                    dve.wait_ge(av_done, PAIRS * b + p - 1)
                dve.tensor_tensor(vs[:, p % 2].rearrange("p t (h k) -> p t h k", h=2),
                                  p_v[:, :].rearrange("p (t h k) -> p t h k", t=KT, h=4)[:, :, 2 * (p % 2):2 * (p % 2) + 2, :],
                                  rdenom[:, p % 2].unsqueeze(3).to_broadcast([P, KT, 2, DK]), ALU.mult).then_inc(v_scaled, 1)

            def expert(b, u, par, first):
                tt, e = UNITS[u]
                n = NU * b + u
                q = u % 2
                dve.wait_ge(h1_copied, n + 1)
                if not (first and u < 2):
                    dve.wait_ge(a_ready, n - 1)
                dve.tensor_tensor(hgl[:, q, :], p_h[:, 2 * P:4 * P], h1[:, q, :], ALU.mult).then_inc(hgl_done, 1)
                dve.wait_ge(hgl_done, n + 1)
                dve.tensor_scalar(gmin[:, q, :], hgl[:, q, 0:P], LIMIT, None, ALU.min).then_inc(g_ready, 1)
                dve.tensor_scalar(lclip[:, q, :], hgl[:, q, P:2 * P], LIMIT, -LIMIT, ALU.min, ALU.max).then_inc(l_ready, 1)
                dve.wait_ge(l_ready, n + 1)
                if u == 0:
                    dve.wait_ge(cw_ready, b + 1)
                dve.tensor_scalar(lscaled[:, q, :], lclip[:, q, :], 1.0, half_cw[:, par, tt, e:e + 1], ALU.add, ALU.mult).then_inc(l_scaled, 1)
                dve.wait_ge(tanh_done, n + 1)
                dve.scalar_tensor_tensor(out=tg[:, q, :], in0=th[:, q, :], scalar=1.0, in1=gmin[:, q, :],
                                         op0=ALU.add, op1=ALU.mult).then_inc(tg_done, 1)
                dve.wait_ge(tg_done, n + 1)
                dve.wait_ge(l_scaled, n + 1)
                if not (first and u < 2):
                    dve.wait_ge(aT_done, n - 1)
                dve.tensor_tensor(act_a[:, q, :], tg[:, q, :], lscaled[:, q, :], ALU.mult).then_inc(a_ready, 1)

            def finish(b, i, par, first):
                dve.wait_ge(wc_done, PAIRS * (b + 1))
                dve.wait_ge(resid_done, b + 1)
                if not (isinstance(i, int) and i == 0):
                    dve.wait_ge(out_stored[par], 16 * i)
                dve.tensor_tensor(yout[par][:, :, :], p_acc[:, 0:L].rearrange("p (t d) -> p t d", t=KT), xres[par][:, :, :],
                                  ALU.add).then_inc(b2_step, 1)
                for e in range(E):
                    dve.wait_ge(b2_step, E * b + e + 1)
                    for tt in range(KT):
                        ins = dve.scalar_tensor_tensor(out=yout[par][:, tt, :], in0=b2_bb[:, e, :], scalar=half_cw[:, par, tt, e:e + 1],
                                                       in1=yout[par][:, tt, :], op0=ALU.mult, op1=ALU.add)
                    ins.then_inc(b2_step, 1) if e < E - 1 else ins.then_inc(y_ready, 1)

            def sequence(i, par, first):
                b = 2 * i + par
                for s in range(STEPS):
                    if s < PAIRS:
                        mask_and_max(b, s, first)
                    for u in units_of(s):
                        expert(b, u, par, first)
                    if s < PAIRS:
                        scale_values(b, s, first)
                finish(b, i, par, first)

            for par in range(2):
                sequence(0, par, par == 0)
            with dve.Fori(1, B // 2) as i:
                for par in range(2):
                    sequence(i, par, False)


_INS = ["source", "Wq", "bq", "Wk", "bk", "Wv", "bv", "Wc", "bc"], ["gate_w", "gate_b", "w1", "b1", "w3", "b3", "w2", "b2",
        "sw1", "sb1", "sw3", "sb3", "sw2", "sb2"]


def kernel(**inputs):
    import numpy as np
    import concourse.bacc as bacc
    from concourse.bass_utils import run_bass_kernel_spmd

    nc = bacc.Bacc("TRN2", target_bir_lowering=False, num_devices=1)
    names = [f"L0_attn_{n}" for n in _INS[0]] + [f"L0_ffn_{n}" for n in _INS[1]]
    arrays = {f"in_{n}": np.ascontiguousarray(inputs[n]) for n in names}
    args = [nc.dram_tensor(n, a.shape, F32, kind="ExternalInput").ap() for n, a in arrays.items()]
    out = nc.dram_tensor("out_0", arrays["in_L0_attn_source"].shape, F32, kind="ExternalOutput").ap()
    build(nc, *args, out)
    return run_bass_kernel_spmd(nc, [arrays], core_ids=[0]).results[0]["out_0"]
```

```python
from contextlib import ExitStack

import numpy as np
import concourse.bass as bass
from concourse import mybir

ALU = mybir.AluOpType
ACT = mybir.ActivationFunctionType
AX = mybir.AxisListType
F32 = mybir.dt.float32
F32R = mybir.dt.float32r
I32 = mybir.dt.int32
U32 = mybir.dt.uint32

P = 128
H, DK = 16, 64
PAIRS = H // 2
STEPS = PAIRS
E = 8
NE = E + 1
LIMIT = 7.0
ALPHA = 1.702
EPS = 1e-5
MASKED = -1e30
GROUP = 4
HALVES = 2
FIRST_R, END_R = 6, 30
R_PER_SEQ = STEPS - 2


def is_int(v):
    return isinstance(v, int)


def units_before(b):
    if is_int(b) and b <= FIRST_R:
        return 2 * b
    if is_int(b) and b > END_R:
        return 2 * FIRST_R + STEPS * (END_R - FIRST_R) + 2 * (b - END_R)
    return STEPS * b - (STEPS - 2) * FIRST_R


def adds_before(b):
    if is_int(b):
        if b <= FIRST_R:
            return max(b - 1, 0)
        n = FIRST_R - 1 + 1 + 3
        if b <= END_R:
            return n + 7 * (b - FIRST_R - 1)
        n += 7 * (END_R - FIRST_R - 1) + 4
        return n + (b - END_R - 1)
    return 7 * b + (FIRST_R + 3 - 7 * (FIRST_R + 1))


def add_index_of_seq(b):
    late = 3 if not is_int(b) or FIRST_R <= b < END_R else 0
    return adds_before(b + 1) + late


def add_index_of_tile(b, j):
    if j >= 3:
        return adds_before(b + 1) + j - 3
    late = 0 if is_int(b) and b == FIRST_R else 3
    return adds_before(b) + late + 1 + j


class Unit:

    def __init__(self, b, s, end):
        if s < 0:
            b, s = b - 1, s + STEPS
        routing = not is_int(b) or FIRST_R <= b < END_R
        there = not is_int(b) or 0 <= b < end
        self.shared = there and s < 2
        self.routed = there and s >= 2 and routing
        self.there = self.shared or self.routed
        self.tt, self.j, self.b = s, s - 2, b
        self.q = s % 2
        if self.there:
            self.n = units_before(b) + s
        if self.routed:
            self.r = R_PER_SEQ * (b - FIRST_R) + self.j


def build(nc, source, Wq, bq, Wk, bk, Wv, bv, Wc, bc, gate_w, gate_b, w1, b1, w3, b3, w2, b2,
          sw1, sb1, sw3, sb3, sw2, sb2, out):
    B, L, D = source.shape
    assert D == P and L == 2 * P
    KT = L // P
    TILES = B * KT
    TOKENS = TILES * P
    GROUPS = TILES // GROUP
    HT = TILES // HALVES
    RT = 2 * HT + E
    assert RT * HALVES == R_PER_SEQ * (END_R - FIRST_R)
    SCALE = float(DK) ** -0.5
    QCOLS = [L - P * kt for kt in range(KT)]
    QOFF = [sum(QCOLS[:kt]) for kt in range(KT)]
    SW = sum(QCOLS)
    HALF_SEQS = B // HALVES
    SCATTERS = 5
    SCATTERS_LATE = 8
    SCATTER_STEPS = -(-2 * HT // SCATTERS)
    SMALL, CONSTS = 6, 7
    RT_CHOSEN, RT_COUNTED, RT_STEPS = 25, 37, 52

    x_rows = source.rearrange("b l d -> (b l) d")
    out_rows = out.rearrange("b l d -> (b l) d")
    xnT_dram = nc.dram_tensor("xnT_dram", (B, P, 2 * L), F32).ap()
    xn_dram = nc.dram_tensor("xn_dram", (TOKENS + P, P), F32).ap()
    sum_dram = nc.dram_tensor("sum_dram", (TOKENS + P, P), F32).ap()
    slots_dram = [nc.dram_tensor(f"slots_dram{h}", (P * RT, 2), I32).ap() for h in range(HALVES)]

    ctx = ExitStack()
    with ctx:
        def sb(name, shape, dt=F32):
            return ctx.enter_context(nc.sbuf_tensor(name, shape, dt))

        def ps(name):
            return ctx.enter_context(nc.psum_tensor(name, [P, 512], F32))

        def sem(name):
            return ctx.enter_context(nc.semaphore(name))

        ident = sb("ident", [P, P])
        mask = sb("mask", [P, L])
        ones2 = sb("ones2", [P, P], F32R)
        before_f = sb("before_f", [P, P])
        before = sb("before", [P, P], F32R)
        ones = sb("ones", [P, P], F32R)
        zeros = sb("zeros", [P, P])
        wqkv = [sb(f"wqkv{part}", [P, 3, H * DK], F32R) for part in range(2)]
        w13 = [sb(f"w13{part}", [P, NE * 4 * P], F32R) for part in range(2)]
        w2T = sb("w2T", [P, NE * P])
        wc = sb("wc", [P, PAIRS, P])
        gateT = [sb(f"gateT{part}", [P, E], F32R) for part in range(2)]
        b13 = sb("b13", [P, NE * 4 * P], F32R)
        b2r = sb("b2r", [P, NE * P], F32R)
        bvr = sb("bvr", [P, H * DK], F32R)
        bqk = sb("bqk", [P, 2, PAIRS])
        gate_bb = sb("gate_bb", [P, E])
        out_bias = sb("out_bias", [P, 3, P])
        raw = sb("raw", [P, 4, 1024])
        bias_rows = [[sb(f"bias13_{k}", [2 * NE, 2 * P], F32R if k else F32), sb(f"bias_v{k}", [H, DK], F32R if k else F32),
                      sb(f"bias2_{k}", [NE, P], F32R if k else F32)] for k in range(3)]
        xs = sb("xs", [P, 2, 2 * GROUP, P])
        stats = sb("stats", [P, 2, 2 * GROUP, 6])
        moments = sb("moments", [P, TILES, 2])
        rstd = sb("rstd", [P, TILES])
        xg = sb("xg", [P, 2, GROUP, P])
        xnT = [sb(f"xnT{part}", [P, 2, GROUP * P], F32R) for part in range(2)]
        logits = sb("logits", [P, TILES, E])
        first_key = sb("first_key", [P, E])
        restart = sb("restart", [P, E, HT])
        tile_no = sb("tile_no", [P, RT])
        token_no = sb("token_no", [P, TILES], I32)
        score = sb("score", [P, HT, E])
        ranked = sb("ranked", [P, HT, E])
        hit = [sb(f"hit{c}", [P, HT, E]) for c in range(2)]
        chosen = sb("chosen", [P, HT, E], F32R)
        scratch = sb("scratch", [P, HT, E])
        count = sb("count", [P, E, HT])
        upto = sb("upto", [P, E, HT])
        red = [sb(f"red{k}", [P, HT]) for k in range(2)]
        weight = [sb(f"weight{c}", [P, HT]) for c in range(2)]
        per_e = [sb(f"per_e{k}", [P, E]) for k in range(4)]
        per_e_i = sb("per_e_i", [P, E], I32)
        end_cmp = sb("end_cmp", [P, RT, E])
        slot_i = [sb(f"slot_i{k}", [P, HT], I32) for k in range(3)]
        slot_f = [sb(f"slot_f{k}", [P, HT]) for k in range(2)]
        pairs = sb("pairs", [P, HALVES, 2, HT, 2], I32)
        slot_row = sb("slot_row", [P, HALVES, 2, HT], U32)
        tile_e = sb("tile_e", [P, RT])
        tile_expert = sb("tile_expert", [P, HALVES * RT], I32)
        slots = sb("slots", [P, HALVES * RT, 2], I32)
        xT = [sb(f"xT{par}", [P, 2, L], F32R) for par in range(2)]
        yout = [sb(f"yout{par}", [P, KT, P]) for par in range(2)]
        qk = sb("qk", [P, 2, 2, L])
        masked_s = sb("masked_s", [P, 2, 2, SW])
        probs = sb("probs", [P, 2, 2, SW])
        neg_max = sb("neg_max", [P, 2, 2, KT])
        denom = sb("denom", [P, 2, KT, 2])
        rdenom = sb("rdenom", [P, 2, KT, 2])
        vs = sb("vs", [P, 2, KT, P])
        headsT = sb("headsT", [P, 2, L])
        slot = sb("slot", [P, R_PER_SEQ, 2], I32)
        xu = sb("xu", [P, 2, P])
        xuT = [sb(f"xuT{part}", [P, 2, P], F32R) for part in range(2)]
        h1 = sb("h1", [P, 2, 2 * P])
        hgl = sb("hgl", [P, 2, 2 * P])
        gmin = sb("gmin", [P, 2, P])
        lclip = sb("lclip", [P, 2, P])
        th = sb("th", [P, 2, P])
        tg = sb("tg", [P, 2, P])
        act_a = sb("act_a", [P, 2, P])
        aT = sb("aT", [P, 2, P])
        yu = sb("yu", [P, 2, P])

        p_qk, p_v, p_s0, p_s1, p_o, p_acc, p_h, p_t = [ps(n) for n in
            ("p_qk", "p_v", "p_s0", "p_s1", "p_o", "p_acc", "p_h", "p_t")]
        p_s = [p_s0, p_s1]

        zeroed = sem("zeroed")
        zeroed_dve = sem("zeroed_dve")
        consts = sem("consts")
        bias_raw_in = sem("bias_raw_in")
        bias_hi = sem("bias_hi")
        bias_lo = sem("bias_lo")
        bias_in = sem("bias_in")
        small_in = sem("small_in")
        raw_qkv_in = sem("raw_qkv_in")
        raw_13_in = [sem(f"raw_13_in{i}") for i in range(2)]
        raw_w2_in = sem("raw_w2_in")
        wT_done = sem("wT_done")
        w2T_ready = sem("w2T_ready")
        wT_hi = sem("wT_hi")
        wT_lo = sem("wT_lo")
        qkv_hi = sem("qkv_hi")
        weights_ready = sem("weights_ready")
        sum_init = sem("sum_init")
        slots_init = sem("slots_init")
        xs_in = [sem(f"xs_in{i}") for i in range(2)]
        stats_done = sem("stats_done")
        moments_done = sem("moments_done")
        std_done = sem("std_done")
        rstd_done = sem("rstd_done")
        xg_in = [sem(f"xg_in{i}") for i in range(2)]
        xn_done = sem("xn_done")
        xn_stored = [sem(f"xn_stored{i}") for i in range(2)]
        xnT_done = sem("xnT_done")
        xnT_hi = sem("xnT_hi")
        xnT_lo = sem("xnT_lo")
        xnT_stored = [sem(f"xnT_stored{i}") for i in range(2)]
        gate_done = sem("gate_done")
        logits_ready = sem("logits_ready")
        rt = sem("rt")
        gate_sub = sem("gate_sub")
        gate_exp = sem("gate_exp")
        counted = sem("counted")
        scattered = [sem(f"scattered{h}") for h in range(HALVES)]
        slots_in = [sem(f"slots_in{h}") for h in range(HALVES)]
        xT_in = [sem(f"xT_in{i}") for i in range(2)]
        qk_proj = sem("qk_proj")
        qk_ready = sem("qk_ready")
        scores_done = sem("scores_done")
        masked = sem("masked")
        probs_ready = sem("probs_ready")
        rdenom_done = sem("rdenom_done")
        v_proj = sem("v_proj")
        v_scaled = sem("v_scaled")
        av_done = sem("av_done")
        heads_ready = sem("heads_ready")
        wc_done = sem("wc_done")
        y_ready = sem("y_ready")
        added = sem("added")
        slot_ready = sem("slot_ready")
        xu_in = [sem(f"xu_in{i}") for i in range(2)]
        xuT_done = sem("xuT_done")
        xuT_hi = sem("xuT_hi")
        xuT_lo = sem("xuT_lo")
        h_done = sem("h_done")
        h1_copied = sem("h1_copied")
        hgl_done = sem("hgl_done")
        g_ready = sem("g_ready")
        l_ready = sem("l_ready")
        tanh_done = sem("tanh_done")
        tg_done = sem("tg_done")
        a_ready = sem("a_ready")
        aT_done = sem("aT_done")
        aT_ready = sem("aT_ready")
        yu_done = sem("yu_done")
        yu_ready = sem("yu_ready")
        out_stored = sem("out_stored")
        waits_apart = sem("waits_apart")

        def apart(eng):
            eng.sem_inc(waits_apart, 1)

        def unit(b, s):
            return Unit(b, s, B)

        def group_at(b, s, late):
            if not is_int(b):
                return None
            k = STEPS * b + s - late
            g = k // 2 + 1
            return g if k >= 0 and k % 2 == 0 and g < GROUPS else None

        def half_at(b, s, late):
            if not is_int(b):
                return None
            for h in range(HALVES):
                if STEPS * b + s == 2 * (GROUPS // HALVES * (h + 1) - 2) + 3 + late:
                    return h
            return None

        def w13_raw(e):
            return raw[:, 2 + e % 2, 0:4 * P].rearrange("p (w u d) -> p w u d", w=2, u=2)

        def w2_raw():
            return raw[:, 0:2, :].rearrange("p a b -> p (a b)")[:, 0:NE * P].rearrange("p (e f) -> p e f", e=NE)

        gate_raw = raw[0:E, 1, 896:1024]
        weight_of_slot = slot[:, :, 1:2].bitcast(F32)

        block = ctx.enter_context(nc.Block())

        def main_loop(eng, sequence):
            for i in range(FIRST_R // 2 + 1):
                for par in range(2):
                    sequence(i, par)
            with eng.Fori(FIRST_R // 2 + 1, END_R // 2) as i:
                for par in range(2):
                    sequence(i, par)
            for i in range(END_R // 2, B // 2):
                for par in range(2):
                    sequence(i, par)

        @block.sync
        def _(sp):
            raw13, rawv, raw2 = bias_rows[0]
            for w, (routed, shared) in enumerate(((b1, sb1), (b3, sb3))):
                sp.dma_start(raw13[w * NE:w * NE + E, :], routed).then_inc(bias_raw_in, 16)
                sp.dma_start(raw13[w * NE + E:w * NE + NE, :], shared.rearrange("(a f) -> a f", a=1)).then_inc(bias_raw_in, 16)
            sp.dma_start(rawv[:, :], bv).then_inc(bias_raw_in, 16)
            sp.dma_start(raw2[0:E, :], b2).then_inc(bias_raw_in, 16)
            sp.dma_start(raw2[E:NE, :], sb2.rearrange("(a f) -> a f", a=1)).then_inc(bias_raw_in, 16)
            for i, w in enumerate((Wq, Wk, Wv)):
                sp.dma_start(raw[:, i, :].rearrange("p (h k) -> p h k", h=H), w.rearrange("h d k -> d h k")).then_inc(raw_qkv_in, 16)
            sp.dma_start(wc[:, :, :], Wc.rearrange("(c p) n -> p c n", p=P)).then_inc(small_in, 16)
            for j, bias in enumerate((bq, bk)):
                sp.dma_start(bqk[:, j, :], bias.rearrange("(c u) k -> (u k) c", u=2), allow_slow_non_contiguous=True).then_inc(small_in, 16)
            sp.dma_start(gate_bb[:, :], gate_b.rearrange("(a e) -> a e", a=1).to_broadcast([P, E])).then_inc(small_in, 16)
            for k, bias in enumerate((bc, sb2)):
                sp.dma_start(out_bias[:, k, :], bias.rearrange("(a e) -> a e", a=1).to_broadcast([P, P])).then_inc(small_in, 16)
            def load_x(g):
                sp.dma_start(xg[:, g % 2], x_rows[g * GROUP * P:(g + 1) * GROUP * P].rearrange("(t p) d -> p t d", p=P)).then_inc(xg_in[g % 2], 16)

            load_x(0)
            load_x(1)
            sp.wait_ge(zeroed, 3)
            sp.wait_ge(bias_hi, 3)
            sp.wait_ge(bias_lo, 3)
            for part, row in enumerate((0, 32)):
                p13, pv, p2 = bias_rows[1 + part]
                for w in range(2):
                    sp.dma_start(b13[row:row + 1, :].bitcast(F32).rearrange("p (e w f) -> p e w f", e=NE, w=2)[:, :, w, :],
                                 p13[w * NE:(w + 1) * NE, :].bitcast(F32)).then_inc(bias_in, 16)
                sp.dma_start(bvr[row:row + 1, :].bitcast(F32).rearrange("p (h k) -> p h k", h=H), pv[:, :].bitcast(F32)).then_inc(bias_in, 16)
                sp.dma_start(b2r[row:row + 1, :].bitcast(F32).rearrange("p (e d) -> p e d", e=NE), p2[:, :].bitcast(F32)).then_inc(bias_in, 16)
            sp.wait_ge(weights_ready, 2)
            for e in range(NE):
                if e >= 2:
                    sp.wait_ge(wT_done, e - 1)
                for w, (routed, shared) in enumerate(((w1, sw1), (w3, sw3))):
                    src = routed[e] if e < E else shared
                    sp.dma_start(w13_raw(e)[:, w], src.rearrange("(u p) d -> p u d", p=P)).then_inc(raw_13_in[e % 2], 16)
                if e == 0:
                    sp.dma_start(w2_raw()[:, 0:E, :], w2.rearrange("e d f -> d e f")).then_inc(raw_w2_in, 16)
                    sp.dma_start(w2_raw()[:, E, :], sw2).then_inc(raw_w2_in, 16)
                    sp.dma_start(gate_raw, gate_w).then_inc(raw_w2_in, 16)
            sp.wait_ge(zeroed_dve, 1)
            sp.dma_start(xn_dram[TOKENS:TOKENS + P, :], zeros[:, :]).then_inc(sum_init, 16)
            sp.dma_start(sum_dram[TOKENS:TOKENS + P, :], zeros[:, :]).then_inc(sum_init, 16)

            def store_xn(g):
                sp.wait_ge(xn_done, g + 1)
                sp.dma_start(xn_dram[g * GROUP * P:(g + 1) * GROUP * P].rearrange("(t p) d -> p t d", p=P), xg[:, g % 2]).then_inc(xn_stored[g % 2], 16)

            def store_xnT(g):
                sp.wait_ge(xnT_lo, g + 1)
                for part in range(2):
                    n = GROUP // KT
                    dst = xnT_dram[g * n:(g + 1) * n].rearrange("s p (a l) -> p s a l", a=2)[:, :, part]
                    sp.dma_start(dst, xnT[part][:, g % 2].bitcast(F32).rearrange("p (s l) -> p s l", l=L)).then_inc(xnT_stored[g % 2], 16)

            def load_seq(b, par):
                sp.dma_start(xT[par][:, :, :].bitcast(F32).rearrange("p a l -> p (a l)"),
                             xnT_dram[bass.ds(b, 1)].rearrange("s p n -> (s p) n")).then_inc(xT_in[par], 16)

            def copy_out(lo, hi):
                def rows(t):
                    return t[lo:hi].rearrange("(a r) d -> a (r d)", a=P)
                sp.dma_start(rows(out_rows), rows(sum_dram)).then_inc(out_stored, 16)

            def load_slots(h):
                sp.wait_ge(scattered[h], 16 * 2 * HT)
                sp.dma_start(slots[:, h * RT:(h + 1) * RT, :].rearrange("p j c -> p (j c)"),
                             slots_dram[h].rearrange("(p j) c -> p (j c)", p=P)).then_inc(slots_in[h], 16)

            store_xn(0)
            store_xnT(0)
            sp.wait_ge(xnT_stored[0], 32)
            load_seq(0, 0)
            load_seq(1, 1)
            for k in range(4):
                lo, hi = k * TOKENS // 4, (k + 1) * TOKENS // 4
                sp.dma_start(sum_dram[lo:hi].rearrange("(a r) d -> a (r d)", a=P), x_rows[lo:hi].rearrange("(a r) d -> a (r d)", a=P)).then_inc(sum_init, 16)

            for b in range(FIRST_R):
                for s in range(STEPS):
                    g = group_at(b, s, 0)
                    if g is not None:
                        if g + 1 < GROUPS:
                            sp.wait_ge(xnT_done, g)
                            sp.wait_ge(xn_stored[(g - 1) % 2], 16 * ((g - 1) // 2 + 1))
                            load_x(g + 1)
                        store_xn(g)
                    g = group_at(b, s, 1)
                    if g is not None:
                        store_xnT(g)
                    h = half_at(b, s, SCATTERS_LATE + SCATTER_STEPS)
                    if h is not None:
                        load_slots(h)
                sp.wait_ge(v_proj, PAIRS // 2 * (b + 1))
                g = (b + 2) // (GROUP // KT)
                sp.wait_ge(xnT_stored[g % 2], 32 * (g // 2 + 1))
                load_seq(b + 2, b % 2)

            load_slots(HALVES - 1)

            def reload(i0, i1):
                with sp.Fori(i0, i1) as i:
                    for par in range(2):
                        sp.wait_ge(v_proj, PAIRS // 2 * (2 * i + par + 1))
                        apart(sp)
                        load_seq(2 * i + par + 2, par)

            last = RT - 1
            done_in = FIRST_R + last // R_PER_SEQ
            need = max(add_index_of_tile(done_in, last % R_PER_SEQ), add_index_of_seq(HALF_SEQS - 1)) + 1
            reload(FIRST_R // 2, done_in // 2 + 1)
            sp.wait_ge(added, 16 * need)
            copy_out(0, TOKENS // HALVES)
            reload(done_in // 2 + 1, B // 2 - 1)
            sp.wait_ge(added, 16 * (add_index_of_seq(END_R - 1) + 1))
            copy_out(TOKENS // HALVES, END_R * L)
            sp.wait_ge(added, 16 * (add_index_of_seq(B - 1) + 1))
            copy_out(END_R * L, TOKENS)
            sp.wait_ge(out_stored, 48)

        @block.gpsimd
        def _(pool):
            for t in (b13, bvr, b2r):
                pool.memset(t[:, :].bitcast(F32), 0.0).then_inc(zeroed, 1)
            pool.memset(ident[:, :], 0.0).then_inc(zeroed, 1)
            pool.memset(mask[:, :], 0.0).then_inc(zeroed, 1)
            pool.memset(before_f[:, :], 1.0).then_inc(zeroed, 1)
            pool.wait_ge(zeroed, 6)
            pool.affine_select(out=ident[:, :], in_=ident[:, :], compare_op=ALU.not_equal, fill=1.0, base=0,
                               pattern=[[-1, P]], channel_multiplier=1).then_inc(consts, 1)
            pool.affine_select(out=mask[:, 0:P], in_=mask[:, 0:P], compare_op=ALU.is_ge, fill=MASKED, base=0,
                               pattern=[[1, P]], channel_multiplier=-1).then_inc(consts, 1)
            pool.affine_select(out=before_f[:, :], in_=before_f[:, :], compare_op=ALU.is_ge, fill=0.0,
                               base=-1, pattern=[[1, P]], channel_multiplier=-1).then_inc(consts, 1)
            pool.iota(token_no[:, :], [[P, TILES]], base=0, channel_multiplier=1).then_inc(consts, 1)
            pool.iota(tile_no[:, :], [[1, RT]], base=0, channel_multiplier=0,
                      allow_small_or_imprecise_dtypes=True).then_inc(consts, 1)
            empty = raw[:, 2, 0:2 * RT].bitcast(I32).rearrange("p (j c) -> p j c", c=2)
            pool.wait_ge(wT_done, NE)
            pool.iota(empty[:, :, 0], [[0, RT]], base=TOKENS, channel_multiplier=1).then_inc(consts, 1)
            pool.memset(empty[:, :, 1], 0).then_inc(consts, 1)
            pool.wait_ge(consts, CONSTS)
            for h in range(HALVES):
                pool.dma_start(slots_dram[h].rearrange("(p j) c -> p (j c)", p=P), empty.rearrange("p j c -> p (j c)")).then_inc(slots_init, 16)

            def scatter_slots(h, part):
                if part == 0:
                    pool.wait_ge(slots_init, 16 * HALVES)
                    pool.wait_ge(rt, RT_STEPS * (h + 1))
                for n in range(part * SCATTERS, min((part + 1) * SCATTERS, 2 * HT)):
                    c, t = divmod(n, HT)
                    pool.indirect_dma_start(
                        out=slots_dram[h][:, :], out_offset=bass.IndirectOffsetOnAxis(ap=slot_row[:, h, c, t:t + 1], axis=0),
                        in_=pairs[:, h, c, t, :], in_offset=None).then_inc(scattered[h], 16)

            def gather(u):
                if is_int(u.r) and u.r in (0, RT):
                    pool.wait_ge(slots_in[u.r // RT], 16)
                if not is_int(u.r) and u.j == 0:
                    pool.wait_ge(slots_in[HALVES - 1], 16)
                if not is_int(u.r) or u.r >= R_PER_SEQ:
                    pool.wait_ge(added, 16 * (add_index_of_tile(u.b - 1, u.j) + 1))
                pool.tensor_copy(slot[:, u.j, :], slots[:, bass.ds(u.r, 1), :].rearrange("p a c -> p (a c)")).then_inc(slot_ready, 1)
                if not is_int(u.r) or u.r >= 2:
                    pool.wait_ge(xuT_done, u.r - 1)
                    apart(pool)
                pool.wait_ge(slot_ready, u.r + 1)
                apart(pool)
                pool.indirect_dma_start(out=xu[:, u.j % 2, :], out_offset=None, in_=xn_dram[:, :],
                                        in_offset=bass.IndirectOffsetOnAxis(ap=slot[:, u.j, 0:1].bitcast(U32), axis=0)).then_inc(xu_in[u.j % 2], 16)

            def before_add(n):
                if is_int(n) and n == 0:
                    pool.wait_ge(sum_init, 16 * 6)
                else:
                    pool.wait_ge(added, 16 * n)
                    apart(pool)

            def add_tile(u):
                pool.wait_ge(yu_ready, u.r + 1)
                apart(pool)
                before_add(add_index_of_tile(u.b, u.j))
                pool.indirect_dma_start(out=sum_dram[:, :], out_offset=bass.IndirectOffsetOnAxis(ap=slot[:, u.j, 0:1].bitcast(U32), axis=0),
                                        in_=yu[:, u.q, :], in_offset=None, compute_op=ALU.add).then_inc(added, 16)

            def add_seq(b, par):
                pool.wait_ge(y_ready, b + 1)
                apart(pool)
                before_add(add_index_of_seq(b))
                pool.dma_start(sum_dram[bass.ds(b * L, L)].rearrange("(t p) d -> p t d", p=P), yout[par][:, :, :],
                               accum_op=ALU.add).then_inc(added, 16)

            def sequence(i, par):
                b = 2 * i + par
                for s in range(STEPS):
                    for part in range(SCATTER_STEPS):
                        h = half_at(b, s, SCATTERS_LATE + part)
                        if h is not None:
                            scatter_slots(h, part)
                    nxt = unit(b, s + 2)
                    if s + 2 < STEPS and nxt.routed:
                        gather(nxt)
                    u = unit(b, s - 3)
                    if u.routed:
                        add_tile(u)
                    if s == 3 and not (is_int(b) and b == 0):
                        add_seq(b - 1, 1 - par)

            main_loop(pool, sequence)
            add_seq(B - 1, 1)

        @block.scalar
        def _(act):
            for i in range(3):
                act.wait_ge(raw_qkv_in, 48)
                act.activation(wqkv[0][:, i, :], raw[:, i, :], ACT.Copy).then_inc(qkv_hi, 1)
            def load_stats(g):
                act.dma_start(xs[:, g % 2], x_rows[g * 2 * GROUP * P:(g + 1) * 2 * GROUP * P].rearrange("(t p) d -> p t d", p=P)).then_inc(xs_in[g % 2], 16)

            for e in range(NE):
                if e < GROUPS // 2:
                    if e >= 2:
                        act.wait_ge(stats_done, e - 1)
                    load_stats(e)
                act.wait_ge(wT_done, e + 1)
                for w in range(2):
                    act.activation(w13[0][:, (4 * e + 2 * w) * P:(4 * e + 2 * w + 2) * P].rearrange("p (two j) -> p two j", two=2),
                                   p_s[e % 2][:, 2 * P * w:2 * P * (w + 1)].rearrange("p (j two) -> p two j", two=2),
                                   ACT.Copy).then_inc(wT_hi, 1)
            for k, bank in enumerate((p_o, p_h, p_t)):
                n = min(4, NE - 4 * k)
                act.wait_ge(wT_done, NE + k + 1)
                act.activation(w2T[:, 4 * k * P:(4 * k + n) * P], bank[:, 0:n * P], ACT.Copy, scale=0.5).then_inc(w2T_ready, 1)
            act.activation(gateT[0][:, :], p_t[:, P:P + E], ACT.Copy).then_inc(wT_hi, 1)
            act.wait_ge(moments_done, 1)
            act.activation(rstd[:, :], rstd[:, :], ACT.Sqrt).then_inc(std_done, 1)

            def split_xnT(g):
                act.wait_ge(xnT_done, g + 1)
                if g >= 2:
                    act.wait_ge(xnT_stored[g % 2], 32 * (g // 2))
                act.activation(xnT[0][:, g % 2, :], p_t[:, :], ACT.Copy).then_inc(xnT_hi, 1)

            def copy_logits(g):
                act.wait_ge(gate_done, g + 1)
                act.activation(logits[:, g * GROUP:(g + 1) * GROUP, :].rearrange("p t e -> p (t e)"), p_t[:, 0:GROUP * E],
                               ACT.Copy).then_inc(logits_ready, 1)

            def qk_evac(b, p):
                act.wait_ge(qk_proj, PAIRS * b + p + 1)
                for j in range(2):
                    ins = act.activation(qk[:, p % 2, j, :], p_qk[:, j * L:(j + 1) * L], ACT.Identity, bias=bqk[:, j, p:p + 1])
                ins.then_inc(qk_ready, 1)

            def exps(b, p, hh):
                if hh == 0 and not (is_int(b) and b == 0 and p < 2):
                    act.wait_ge(av_done, PAIRS * b + p - 1)
                act.wait_ge(masked, 2 * (PAIRS * b + p) + hh + 1)
                for kt in range(KT):
                    cols = slice(QOFF[kt], QOFF[kt] + QCOLS[kt])
                    ins = act.activation(probs[:, p % 2, hh, cols], masked_s[:, p % 2, hh, cols], ACT.Exp,
                                         bias=neg_max[:, p % 2, hh, kt:kt + 1], scale=-1.0,
                                         accum_out=denom[:, p % 2, kt, hh:hh + 1])
                ins.then_inc(probs_ready, 1)

            def heads_evac(b, p):
                act.wait_ge(av_done, PAIRS * b + p + 1)
                if not (is_int(b) and b == 0 and p < 2):
                    act.wait_ge(wc_done, PAIRS * b + p - 1)
                act.activation(headsT[:, p % 2, :], p_o[:, 0:L], ACT.Copy).then_inc(heads_ready, 1)

            def split_xu(u):
                act.wait_ge(xuT_done, u.r + 1)
                act.activation(xuT[0][:, u.q, :], p_o[:, L:L + P], ACT.Copy).then_inc(xuT_hi, 1)

            def copy_h1(u):
                act.wait_ge(h_done, u.n + 1)
                act.activation(h1[:, u.q, :], p_h[:, 0:2 * P], ACT.Copy).then_inc(h1_copied, 1)

            def tanh(u):
                act.wait_ge(g_ready, u.n + 1)
                act.activation(th[:, u.q, :], gmin[:, u.q, :], ACT.Tanh, scale=ALPHA / 2).then_inc(tanh_done, 1)

            def evac_aT(u):
                act.wait_ge(aT_done, u.n + 1)
                act.activation(aT[:, u.q, :], p_t[:, P:2 * P], ACT.Copy).then_inc(aT_ready, 1)

            def weigh(u):
                act.wait_ge(yu_done, u.r + 1)
                if not is_int(u.r) or u.r >= 2:
                    b, j = (u.b, u.j - 2) if u.j >= 2 else (u.b - 1, u.j + R_PER_SEQ - 2)
                    act.wait_ge(added, 16 * (add_index_of_tile(b, j) + 1))
                act.activation(yu[:, u.q, :], p_t[:, 2 * P:3 * P], ACT.Copy, scale=weight_of_slot[:, u.j, :]).then_inc(yu_ready, 1)

            def sequence(i, par):
                b = 2 * i + par
                for s in range(STEPS):
                    if s + 1 < PAIRS:
                        qk_evac(b, s + 1)
                    elif not (is_int(b) and b == B - 1):
                        qk_evac(b + 1, 0)
                    exps(b, s, 0)
                    u = unit(b, s + 1)
                    if s + 1 < STEPS and u.routed:
                        split_xu(u)
                    if unit(b, s - 1).there:
                        evac_aT(unit(b, s - 1))
                    if unit(b, s).there:
                        copy_h1(unit(b, s))
                    exps(b, s, 1)
                    if unit(b, s).there:
                        tanh(unit(b, s))
                    if unit(b, s - 2).routed:
                        weigh(unit(b, s - 2))
                    if not (is_int(b) and b == 0 and s == 0):
                        heads_evac(*((b, s - 1) if s else (b - 1, PAIRS - 1)))
                    g = group_at(b, s, 1)
                    if g is not None:
                        split_xnT(g)
                    g = group_at(b, s, 2)
                    if g is not None:
                        copy_logits(g)
                    h = half_at(b, s, 1)
                    if h is not None:
                        act.wait_ge(gate_sub, h + 1)
                        act.activation(score[:, :, :], score[:, :, :], ACT.Exp).then_inc(gate_exp, 1)

            split_xnT(0)
            copy_logits(0)
            qk_evac(0, 0)
            main_loop(act, sequence)
            heads_evac(B - 1, PAIRS - 1)

        @block.tensor
        def _(pe):
            def three(dst, stat, mov, start, stop, **kw):
                pe.matmul(dst, stat[0], mov[0], start=start, stop=False, **kw)
                pe.matmul(dst, stat[1], mov[0], start=False, stop=False, **kw)
                return pe.matmul(dst, stat[0], mov[1], start=False, stop=stop, **kw)

            pe.wait_ge(consts, 3)
            for e in range(NE):
                pe.wait_ge(raw_13_in[e % 2], 32 * (e // 2 + 1))
                if e >= 2:
                    pe.wait_ge(wT_lo, e - 1)
                for w in range(2):
                    for u in range(2):
                        ins = pe.transpose(p_s[e % 2][:, (2 * w + u) * P:(2 * w + u + 1) * P], w13_raw(e)[:, w, u, :], ident[:, :])
                ins.then_inc(wT_done, 1)
            pe.wait_ge(raw_w2_in, 48)
            for k, bank in enumerate((p_o, p_h, p_t)):
                for e in range(4 * k, min(4 * k + 4, NE)):
                    ins = pe.transpose(bank[:, (e % 4) * P:(e % 4 + 1) * P], w2_raw()[:, e, :], ident[:, :])
                if k == 2:
                    ins = pe.transpose(p_t[:, P:P + E], gate_raw, ident[0:E, 0:E])
                ins.then_inc(wT_done, 1)

            def wait_turned(b, s):
                if STEPS * b + s >= 1:
                    pe.wait_ge(aT_ready, units_before(b) + min(s, 2))

            def turn_xn(g, b, s):
                pe.wait_ge(xn_done, g + 1)
                if g >= 1:
                    pe.wait_ge(logits_ready, g)
                wait_turned(b, s)
                for t in range(GROUP):
                    ins = pe.transpose(p_t[:, t * P:(t + 1) * P], xg[:, g % 2, t, :], ident[:, :])
                ins.then_inc(xnT_done, 1)

            def gate(g, b, s):
                pe.wait_ge(xnT_lo, g + 1)
                wait_turned(b, s)
                for t in range(GROUP):
                    cols = slice(t * P, (t + 1) * P)
                    ins = three(p_t[:, t * E:(t + 1) * E], [xnT[k][:, g % 2, cols] for k in range(2)],
                                [gateT[k][:, :] for k in range(2)], start=True, stop=True, skip_group_check=True)
                ins.then_inc(gate_done, 1)

            def count_tokens(h, b):
                pe.wait_ge(hgl_done, units_before(b + 1))
                pe.wait_ge(rt, RT_STEPS * h + RT_CHOSEN)
                m = chosen[:, :, :].rearrange("p t e -> p (t e)")
                pe.matmul(p_h[:, 0:HT * E], before[:, :], m, start=True, stop=True, skip_group_check=True)
                pe.matmul(p_h[:, HT * E:2 * HT * E], ones[:, :], m, start=True, stop=True, skip_group_check=True).then_inc(counted, 1)

            def turn_xu(u, b, s):
                pe.wait_ge(xu_in[u.j % 2], 16 * ((u.r - u.j % 2) // 2 + 1) if is_int(u.r) else 8 * (u.r - u.j % 2) + 16)
                pe.wait_ge(heads_ready, PAIRS * b + s - 1)
                pe.transpose(p_o[:, L:L + P], xu[:, u.j % 2, :], ident[:, :]).then_inc(xuT_done, 1)

            def unit_in(u, par):
                if not (is_int(u.n) and u.n == 0):
                    pe.wait_ge(hgl_done, u.n)
                for h in range(HALVES):
                    if u.tt == 0 and is_int(u.b) and h in [half_at(u.b - 1, s, 5) for s in range(2, STEPS)]:
                        pe.wait_ge(rt, RT_STEPS * h + RT_COUNTED)
                if u.shared:
                    stat = [xT[par][:, k, u.tt * P:(u.tt + 1) * P] for k in range(2)]
                    w, bias = [w[:, E * 4 * P:] for w in w13], b13[:, E * 4 * P:]
                else:
                    pe.wait_ge(xuT_lo, u.r + 1)
                    stat = [xuT[k][:, u.q, :] for k in range(2)]
                    at = bass.ds(expert[u.j] * (4 * P), 4 * P)
                    w, bias = [w[:, at] for w in w13], b13[:, at]
                three(p_h[:, :], stat, w, start=True, stop=False)
                pe.matmul(p_h[:, :], ones2[:, :], bias, start=False, stop=True).then_inc(h_done, 1)

            def unit_turn(u, b, s):
                pe.wait_ge(a_ready, u.n + 1)
                g = group_at(b, s, 2)
                if g is not None:
                    pe.wait_ge(xnT_lo, g + 1)
                g = group_at(b, s, 3)
                if g is not None:
                    pe.wait_ge(logits_ready, g + 1)
                if unit(b, s - 3).routed:
                    pe.wait_ge(yu_ready, unit(b, s - 3).r + 1)
                pe.transpose(p_t[:, P:2 * P], act_a[:, u.q, :], ident[:, :]).then_inc(aT_done, 1)

            def unit_out(u, b, s):
                pe.wait_ge(aT_ready, u.n + 1)
                nxt = unit(b, s - 1)
                if nxt.there:
                    pe.wait_ge(aT_ready, nxt.n + 1)
                if u.shared:
                    pe.matmul(p_acc[:, u.tt * P:(u.tt + 1) * P], aT[:, u.q, :], w2T[:, E * P:], start=False, stop=False,
                              skip_group_check=True)
                else:
                    at = bass.ds(expert[u.j] * P, P)
                    dst = p_t[:, 2 * P:3 * P]
                    pe.matmul(dst, aT[:, u.q, :], w2T[:, at], start=True, stop=False, skip_group_check=True)
                    pe.matmul(dst, ones2[:, :], b2r[:, at], start=False, stop=True, skip_group_check=True).then_inc(yu_done, 1)

            def project_qk(b, p, par):
                if p == 0:
                    pe.wait_ge(xT_in[par], 16 * ((b - par) // 2 + 1) if is_int(b) else 8 * (b - par) + 16)
                if not (is_int(b) and b == 0 and p == 0):
                    pe.wait_ge(qk_ready, PAIRS * b + p)
                for j in range(2):
                    ins = three(p_qk[:, j * L:(j + 1) * L], [w[:, j, p * P:(p + 1) * P] for w in wqkv],
                                [xT[par][:, k, :] for k in range(2)], start=True, stop=True)
                ins.then_inc(qk_proj, 1)

            def scores(b, p):
                pe.wait_ge(qk_ready, PAIRS * b + p + 1)
                for hh in range(2):
                    if not (is_int(b) and b == 0 and p == 0):
                        pe.wait_ge(masked, 2 * (PAIRS * b + p) + hh - 1)
                    rows = slice(DK * hh, DK * (hh + 1))
                    for kt in range(KT):
                        ins = pe.matmul(p_s[hh][:, QOFF[kt]:QOFF[kt] + QCOLS[kt]],
                                        qk[rows, p % 2, 1, kt * P:(kt + 1) * P], qk[rows, p % 2, 0, kt * P:L],
                                        start=True, stop=True, skip_group_check=True)
                    ins.then_inc(scores_done, 1)

            def project_v(b, g, par):
                if not (is_int(b) and b == 0 and g == 0):
                    pe.wait_ge(v_scaled, PAIRS * b + 2 * g)
                cols = slice(g * 2 * P, (g + 1) * 2 * P)
                for kt in range(KT):
                    dst = p_v[:, kt * 2 * P:(kt + 1) * 2 * P]
                    three(dst, [xT[par][:, k, kt * P:(kt + 1) * P] for k in range(2)],
                          [w[:, 2, cols] for w in wqkv], start=True, stop=False)
                    ins = pe.matmul(dst, ones2[:, :], bvr[:, cols], start=False, stop=True)
                ins.then_inc(v_proj, 1)

            def values(b, p, turned):
                pe.wait_ge(v_scaled, PAIRS * b + p + 1)
                if turned:
                    pe.wait_ge(xuT_lo, turned.r + 1)
                if not (is_int(b) and b == 0 and p == 0):
                    pe.wait_ge(heads_ready, PAIRS * b + p)
                for kt in range(KT):
                    for hh in range(2):
                        rows = slice(DK * hh, DK * (hh + 1))
                        ins = pe.matmul(p_o[rows, kt * P:L], vs[:, p % 2, kt, rows],
                                        probs[:, p % 2, hh, QOFF[kt]:QOFF[kt] + QCOLS[kt]],
                                        start=(kt == 0), stop=(kt == KT - 1), skip_group_check=True)
                ins.then_inc(av_done, 1)

            def out_projection(b, p):
                pe.wait_ge(heads_ready, PAIRS * b + p + 1)
                if p == 0 and not (is_int(b) and b == 0):
                    pe.wait_ge(y_ready, b)
                for tt in range(KT):
                    ins = pe.matmul(p_acc[:, tt * P:(tt + 1) * P], headsT[:, p % 2, tt * P:(tt + 1) * P], wc[:, p, :],
                                    start=(p == 0 and tt == 0), stop=False, skip_group_check=True)
                ins.then_inc(wc_done, 1)

            def pair_before(b, s, late):
                if s >= late:
                    return b, s - late
                return None if is_int(b) and b == 0 else (b - 1, s - late + PAIRS)

            expert = [None] * R_PER_SEQ

            def load_expert(r, j):
                expert[j] = pe.value_load(tile_expert[0:1, bass.ds(r, 1)], min_val=0, max_val=E - 1)

            def sequence(i, par):
                b = 2 * i + par
                r0 = R_PER_SEQ * (b - FIRST_R)
                for s in range(STEPS):
                    scores(b, s)
                    u, out_u, nxt = unit(b, s), unit(b, s - 2), unit(b, s + 1)
                    if s + 1 == STEPS or not nxt.routed:
                        nxt = None
                    if u.routed:
                        if is_int(u.r) and u.r % RT == 0:
                            pe.wait_ge(rt, RT_STEPS * (u.r // RT + 1))
                        load_expert(u.r, u.j)
                    if out_u.routed and s < 2:
                        load_expert(out_u.r, out_u.j)
                    if nxt:
                        turn_xu(nxt, b, s)
                    if unit(b, s - 1).there:
                        unit_turn(unit(b, s - 1), b, s)
                    if u.there:
                        unit_in(u, par)
                    if s % 2 == 0:
                        project_v(b, s // 2, par)
                    if s + 2 < PAIRS:
                        project_qk(b, s + 2, par)
                    elif not (is_int(b) and b == B - 1):
                        project_qk(b + 1, s + 2 - PAIRS, 1 - par)
                    if pair_before(b, s, 2):
                        out_projection(*pair_before(b, s, 2))
                    if out_u.there:
                        unit_out(out_u, b, s)
                    g = group_at(b, s, 1)
                    if g is not None:
                        turn_xn(g, b, s)
                    g = group_at(b, s, 2)
                    if g is not None:
                        gate(g, b, s)
                    h = half_at(b, s, 5)
                    if h is not None:
                        count_tokens(h, b)
                    if pair_before(b, s, 1):
                        values(*pair_before(b, s, 1), nxt)

            turn_xn(0, 0, 0)
            gate(0, 0, 0)
            pe.wait_ge(weights_ready, 3)
            pe.wait_ge(bias_in, 16 * 8)
            pe.wait_ge(small_in, 16 * SMALL)
            pe.wait_ge(logits_ready, 1)
            project_qk(0, 0, 0)
            project_qk(0, 1, 0)
            main_loop(pe, sequence)
            out_projection(B - 1, PAIRS - 2)
            values(B - 1, PAIRS - 1, None)
            out_projection(B - 1, PAIRS - 1)

        @block.vector
        def _(dve):
            dve.memset(zeros[:, :], 0.0).then_inc(zeroed_dve, 1)
            dve.memset(ones2[:, :].bitcast(F32), 0.0).then_inc(zeroed_dve, 1)
            dve.wait_ge(zeroed_dve, 2)
            for row in (0, 32):
                dve.memset(ones2[row:row + 1, :].bitcast(F32), 1.0)
            dve.memset(ones[:, :].bitcast(F32), 1.0)
            for e in range(E):
                dve.memset(first_key[:, e:e + 1], float(E - e))
            dve.memset(restart[:, :, 1:], 1.0)
            dve.memset(restart[:, :, 0:1], 0.0).then_inc(weights_ready, 1)
            dve.wait_ge(bias_raw_in, 16 * 7)

            def by_parity(t, k):
                return t[:, :].rearrange("p (j two) -> p two j", two=2) if k == 0 else t[:, :]

            def as_parity(t, k):
                return t[:, :].rearrange("p (two j) -> p two j", two=2) if k == 0 else t[:, :]

            for k in range(3):
                dve.tensor_copy(as_parity(bias_rows[1][k], k), by_parity(bias_rows[0][k], k)).then_inc(bias_hi, 1)
            for k in range(3):
                dve.wait_ge(bias_hi, k + 1)
                dve.tensor_tensor(as_parity(bias_rows[2][k], k), by_parity(bias_rows[0][k], k), as_parity(bias_rows[1][k], k).bitcast(F32),
                                  ALU.subtract).then_inc(bias_lo, 1)
            for i in range(3):
                dve.wait_ge(qkv_hi, i + 1)
                ins = dve.tensor_tensor(wqkv[1][:, i, :], raw[:, i, :], wqkv[0][:, i, :].bitcast(F32), ALU.subtract)
            ins.then_inc(weights_ready, 1)
            dve.wait_ge(consts, 3)
            dve.tensor_copy(before[:, :], before_f[:, :])
            dve.wait_ge(small_in, 16 * SMALL)
            dve.tensor_tensor(out_bias[:, 2, :], out_bias[:, 0, :], out_bias[:, 1, :], ALU.add)

            def statistics(g):
                dve.wait_ge(xs_in[g % 2], 16 * (g // 2 + 1))
                for t in range(2 * GROUP):
                    ins = dve.bn_stats(stats[:, g % 2, t, :], xs[:, g % 2, t, :])
                ins.then_inc(stats_done, 1)
                dve.wait_ge(stats_done, g + 1)
                for t in range(2 * GROUP):
                    ins = dve.bn_aggr(moments[:, 2 * GROUP * g + t, :], stats[:, g % 2, t, :])
                return ins

            for e in range(NE):
                dve.wait_ge(wT_hi, 2 * e + 2)
                for w in range(2):
                    def halves(t):
                        return t[:, (4 * e + 2 * w) * P:(4 * e + 2 * w + 2) * P].rearrange("p (two j) -> p two j", two=2)
                    ins = dve.tensor_tensor(halves(w13[1]), p_s[e % 2][:, 2 * P * w:2 * P * (w + 1)].rearrange("p (j two) -> p two j", two=2),
                                            halves(w13[0]).bitcast(F32), ALU.subtract)
                ins.then_inc(wT_lo, 1)
                if e < GROUPS // 2:
                    ins = statistics(e)
                    if e == GROUPS // 2 - 1:
                        ins.then_inc(rstd_done, 1)
            dve.wait_ge(wT_hi, 2 * NE + 1)
            dve.tensor_tensor(gateT[1][:, :], p_t[:, P:P + E], gateT[0][:, :].bitcast(F32), ALU.subtract).then_inc(weights_ready, 1)
            dve.wait_ge(rstd_done, 1)
            dve.tensor_scalar(rstd[:, :], moments[:, :, 1], EPS, None, ALU.add).then_inc(moments_done, 1)
            dve.wait_ge(std_done, 1)
            dve.reciprocal(rstd[:, :], rstd[:, :]).then_inc(rstd_done, 1)
            dve.wait_ge(rstd_done, 2)

            def normalise(g):
                dve.wait_ge(xg_in[g % 2], 16 * (g // 2 + 1))
                for t in range(GROUP):
                    n = g * GROUP + t
                    ins = dve.tensor_scalar(xg[:, g % 2, t, :], xg[:, g % 2, t, :], moments[:, n, 0:1], rstd[:, n:n + 1],
                                            ALU.subtract, ALU.mult)
                ins.then_inc(xn_done, 1)

            def split_xnT(g):
                dve.wait_ge(xnT_hi, g + 1)
                if g >= 2:
                    dve.wait_ge(xnT_stored[g % 2], 32 * (g // 2))
                dve.tensor_tensor(xnT[1][:, g % 2, :], p_t[:, :], xnT[0][:, g % 2, :].bitcast(F32), ALU.subtract).then_inc(xnT_lo, 1)

            k = [0]

            def then(ins):
                k[0] += 1
                ins.then_inc(rt, 1)
                dve.wait_ge(rt, k[0])

            def over_experts(t):
                return t[:, :].unsqueeze(2).to_broadcast([P, HT, E])

            def subtract_max(h):
                lg = logits[:, h * HT:(h + 1) * HT, :]
                dve.wait_ge(logits_ready, GROUPS // HALVES * (h + 1))
                then(dve.tensor_reduce(red[0][:, :], lg, AX.X, ALU.max))
                dve.tensor_tensor(score[:, :, :], lg, over_experts(red[0]), ALU.subtract).then_inc(gate_sub, 1)

            def gate_softmax(h):
                dve.wait_ge(consts, CONSTS)
                dve.wait_ge(gate_exp, h + 1)
                then(dve.tensor_reduce(red[0][:, :], score[:, :, :], AX.X, ALU.add))
                then(dve.reciprocal(red[1][:, :], red[0][:, :]))
                then(dve.tensor_tensor(score[:, :, :], score[:, :, :], over_experts(red[1]), ALU.mult))
                then(dve.tensor_tensor(ranked[:, :, :], score[:, :, :], gate_bb[:, :].unsqueeze(1).to_broadcast([P, HT, E]), ALU.add))

            def choose(h, c):
                keys = first_key[:, :].unsqueeze(1).to_broadcast([P, HT, E])
                then(dve.tensor_reduce(red[0][:, :], ranked[:, :, :], AX.X, ALU.max))
                then(dve.tensor_tensor(scratch[:, :, :], ranked[:, :, :], over_experts(red[0]), ALU.is_equal))
                then(dve.tensor_tensor(scratch[:, :, :], scratch[:, :, :], keys, ALU.mult))
                then(dve.tensor_reduce(red[0][:, :], scratch[:, :, :], AX.X, ALU.max))
                then(dve.tensor_tensor(hit[c][:, :, :], keys, over_experts(red[0]), ALU.is_equal))
                if c == 0:
                    then(dve.scalar_tensor_tensor(out=ranked[:, :, :], in0=hit[0][:, :, :], scalar=MASKED, in1=ranked[:, :, :],
                                                  op0=ALU.mult, op1=ALU.add))
                then(dve.tensor_tensor(scratch[:, :, :], hit[c][:, :, :], score[:, :, :], ALU.mult))
                then(dve.tensor_reduce(weight[c][:, :], scratch[:, :, :], AX.X, ALU.add))
                then(dve.tensor_copy(pairs[:, h, c, :, 1].bitcast(F32), weight[c][:, :]))
                then(dve.tensor_copy(pairs[:, h, c, :, 0], token_no[:, h * HT:(h + 1) * HT]))

            def choose_first(h):
                choose(h, 0)

            def choose_second(h):
                choose(h, 1)
                then(dve.tensor_tensor(chosen[:, :, :], hit[0][:, :, :], hit[1][:, :, :], ALU.add))
                assert k[0] == RT_STEPS * h + RT_CHOSEN, k[0]

            def place(h):
                dve.wait_ge(counted, h + 1)
                then(dve.tensor_copy(count[:, :, :], p_h[:, HT * E:2 * HT * E].rearrange("p (t e) -> p e t", e=E)))
                then(dve.tensor_tensor_scan(upto[:, :, :].rearrange("p e t -> p (e t)"), restart[:, :, :].rearrange("p e t -> p (e t)"),
                                            count[:, :, :].rearrange("p e t -> p (e t)"), 0.0, ALU.mult, ALU.add))
                then(dve.tensor_scalar(per_e_i[:, :], upto[:, :, HT - 1], float(P - 1), None, ALU.add))
                then(dve.tensor_single_scalar(per_e_i[:, :], per_e_i[:, :], 7, ALU.arith_shift_right))
                then(dve.tensor_copy(per_e[0][:, :], per_e_i[:, :]))
                then(dve.memset(per_e[1][:, :], 1.0))
                then(dve.tensor_tensor_scan(per_e[2][:, :], per_e[1][:, :], per_e[0][:, :], 0.0, ALU.mult, ALU.add))
                then(dve.tensor_tensor(per_e[3][:, :], per_e[2][:, :], per_e[0][:, :], ALU.subtract))
                then(dve.tensor_scalar(per_e[3][:, :], per_e[3][:, :], float(P), None, ALU.mult))
                then(dve.tensor_tensor(upto[:, :, :], upto[:, :, :], count[:, :, :], ALU.subtract))
                then(dve.tensor_tensor(upto[:, :, :], upto[:, :, :], per_e[3][:, :].unsqueeze(2).to_broadcast([P, E, HT]), ALU.add))
                then(dve.tensor_tensor(ranked[:, :, :], p_h[:, 0:HT * E].rearrange("p (t e) -> p t e", e=E),
                                       upto[:, :, :].rearrange("p e t -> p t e"), ALU.add))
                assert k[0] == RT_STEPS * h + RT_COUNTED, k[0]

            def place_choice(h, c):
                then(dve.tensor_tensor(scratch[:, :, :], hit[c][:, :, :], ranked[:, :, :], ALU.mult))
                then(dve.tensor_reduce(slot_f[0][:, :], scratch[:, :, :], AX.X, ALU.add))
                then(dve.tensor_copy(slot_i[0][:, :], slot_f[0][:, :]))
                then(dve.tensor_single_scalar(slot_i[1][:, :], slot_i[0][:, :], P - 1, ALU.bitwise_and))
                then(dve.tensor_single_scalar(slot_i[2][:, :], slot_i[0][:, :], 7, ALU.arith_shift_right))
                then(dve.scalar_tensor_tensor(out=slot_row[:, h, c, :], in0=slot_i[1][:, :], scalar=float(RT), in1=slot_i[2][:, :],
                                              op0=ALU.mult, op1=ALU.add))

            def place_first(h):
                place_choice(h, 0)

            def place_second(h):
                place_choice(h, 1)
                then(dve.tensor_tensor(end_cmp[:, :, :], tile_no[:, :].unsqueeze(2).to_broadcast([P, RT, E]),
                                       per_e[2][:, :].unsqueeze(1).to_broadcast([P, RT, E]), ALU.is_ge))
                then(dve.tensor_reduce(tile_e[:, :], end_cmp[:, :, :], AX.X, ALU.add))
                then(dve.tensor_scalar(tile_expert[:, h * RT:(h + 1) * RT], tile_e[:, :], float(E - 1), None, ALU.min))
                assert k[0] == RT_STEPS * (h + 1), k[0]

            routing_stages = (subtract_max, None, gate_softmax, choose_first, choose_second, place, place_first, place_second)

            def mask_and_max(b, p):
                for hh in range(2):
                    if hh == 0 and not (is_int(b) and b == 0 and p < 2):
                        dve.wait_ge(probs_ready, 2 * (PAIRS * b + p - 1))
                        apart(dve)
                    dve.wait_ge(scores_done, 2 * (PAIRS * b + p) + hh + 1)
                    apart(dve)
                    for kt in range(KT):
                        cols = slice(QOFF[kt], QOFF[kt] + QCOLS[kt])
                        ins = dve.tensor_tensor_reduce(out=masked_s[:, p % 2, hh, cols], in0=p_s[hh][:, cols],
                                                       in1=mask[:, 0:QCOLS[kt]], scale=-SCALE, scalar=-MASKED,
                                                       op0=ALU.add, op1=ALU.min, accum_out=neg_max[:, p % 2, hh, kt:kt + 1])
                    ins.then_inc(masked, 1)

            def scale_values(b, p):
                dve.wait_ge(probs_ready, 2 * (PAIRS * b + p) + 2)
                dve.reciprocal(rdenom[:, p % 2], denom[:, p % 2]).then_inc(rdenom_done, 1)
                dve.wait_ge(rdenom_done, PAIRS * b + p + 1)
                dve.wait_ge(v_proj, PAIRS // 2 * b + p // 2 + 1)
                if not (is_int(b) and b == 0 and p < 2):
                    dve.wait_ge(av_done, PAIRS * b + p - 1)
                dve.tensor_tensor(vs[:, p % 2].rearrange("p t (h k) -> p t h k", h=2),
                                  p_v[:, :].rearrange("p (t h k) -> p t h k", t=KT, h=4)[:, :, 2 * (p % 2):2 * (p % 2) + 2, :],
                                  rdenom[:, p % 2].unsqueeze(3).to_broadcast([P, KT, 2, DK]), ALU.mult).then_inc(v_scaled, 1)

            def split_xu(u):
                dve.wait_ge(xuT_hi, u.r + 1)
                dve.tensor_tensor(xuT[1][:, u.q, :], p_o[:, L:L + P], xuT[0][:, u.q, :].bitcast(F32), ALU.subtract).then_inc(xuT_lo, 1)

            def unit_product(u):
                dve.wait_ge(h1_copied, u.n + 1)
                dve.tensor_tensor(hgl[:, u.q, :], p_h[:, 2 * P:4 * P], h1[:, u.q, :], ALU.mult).then_inc(hgl_done, 1)
                dve.wait_ge(hgl_done, u.n + 1)
                dve.tensor_scalar(gmin[:, u.q, :], hgl[:, u.q, 0:P], LIMIT, None, ALU.min).then_inc(g_ready, 1)
                dve.tensor_scalar(lclip[:, u.q, :], hgl[:, u.q, P:2 * P], LIMIT, -LIMIT, ALU.min, ALU.max).then_inc(l_ready, 1)

            def unit_gate(u):
                dve.wait_ge(tanh_done, u.n + 1)
                dve.scalar_tensor_tensor(out=tg[:, u.q, :], in0=th[:, u.q, :], scalar=1.0, in1=gmin[:, u.q, :],
                                         op0=ALU.add, op1=ALU.mult).then_inc(tg_done, 1)
                dve.wait_ge(tg_done, u.n + 1)
                if not (is_int(u.n) and u.n < 2):
                    dve.wait_ge(aT_done, u.n - 1)
                dve.scalar_tensor_tensor(out=act_a[:, u.q, :], in0=lclip[:, u.q, :], scalar=1.0, in1=tg[:, u.q, :],
                                         op0=ALU.add, op1=ALU.mult).then_inc(a_ready, 1)

            def finish(b, par):
                dve.wait_ge(wc_done, PAIRS * (b + 1))
                if not (is_int(b) and b < 2):
                    dve.wait_ge(added, 16 * (add_index_of_seq(b - 2) + 1))
                dve.tensor_tensor(yout[par][:, :, :], p_acc[:, 0:L].rearrange("p (t d) -> p t d", t=KT),
                                  out_bias[:, 2, :].unsqueeze(1).to_broadcast([P, KT, P]), ALU.add).then_inc(y_ready, 1)

            def sequence(i, par):
                b = 2 * i + par
                for s in range(STEPS):
                    if s == 2 and not (is_int(b) and b == 0):
                        finish(b - 1, 1 - par)
                    mask_and_max(b, s)
                    if s + 1 < STEPS and unit(b, s + 1).routed:
                        split_xu(unit(b, s + 1))
                    if unit(b, s).there:
                        unit_product(unit(b, s))
                    scale_values(b, s)
                    if unit(b, s).there:
                        unit_gate(unit(b, s))
                    g = group_at(b, s, 0)
                    if g is not None:
                        normalise(g)
                    g = group_at(b, s, 1)
                    if g is not None:
                        split_xnT(g)
                    for late, stage in enumerate(routing_stages):
                        h = half_at(b, s, late)
                        if h is not None and stage:
                            stage(h)

            normalise(0)
            split_xnT(0)
            main_loop(dve, sequence)
            finish(B - 1, 1)


_INS = ["source", "Wq", "bq", "Wk", "bk", "Wv", "bv", "Wc", "bc"], ["gate_w", "gate_b", "w1", "b1", "w3", "b3", "w2", "b2",
        "sw1", "sb1", "sw3", "sb3", "sw2", "sb2"]


def kernel(**inputs):
    import numpy as np
    import concourse.bacc as bacc
    from concourse.bass_utils import run_bass_kernel_spmd

    nc = bacc.Bacc("TRN2", target_bir_lowering=False, num_devices=1)
    names = [f"L0_attn_{n}" for n in _INS[0]] + [f"L0_ffn_{n}" for n in _INS[1]]
    arrays = {f"in_{n}": np.ascontiguousarray(inputs[n]) for n in names}
    args = [nc.dram_tensor(n, a.shape, F32, kind="ExternalInput").ap() for n, a in arrays.items()]
    out = nc.dram_tensor("out_0", arrays["in_L0_attn_source"].shape, F32, kind="ExternalOutput").ap()
    build(nc, *args, out)
    return run_bass_kernel_spmd(nc, [arrays], core_ids=[0]).results[0]["out_0"]
```

```python
from contextlib import ExitStack

import numpy as np
import concourse.bass as bass
from concourse import mybir

ALU = mybir.AluOpType
ACT = mybir.ActivationFunctionType
AX = mybir.AxisListType
F32 = mybir.dt.float32
F32R = mybir.dt.float32r
I32 = mybir.dt.int32
U32 = mybir.dt.uint32

P = 128
H, DK = 16, 64
PAIRS = H // 2
STEPS = PAIRS
E = 8
NE = E + 1
LIMIT = 7.0
ALPHA = 1.702
EPS = 1e-5
MASKED = -1e30
GROUP = 4
XS = 3
HALVES = 2
FIRST_R, END_R = 6, 30
R_PER_SEQ = STEPS - 2


def is_int(v):
    return isinstance(v, int)


def units_before(b):
    if is_int(b) and b <= FIRST_R:
        return 2 * b
    if is_int(b) and b > END_R:
        return 2 * FIRST_R + STEPS * (END_R - FIRST_R) + 2 * (b - END_R)
    return STEPS * b - (STEPS - 2) * FIRST_R


def adds_before(b):
    if is_int(b):
        if b <= FIRST_R:
            return max(b - 1, 0)
        n = FIRST_R - 1 + 1 + 3
        if b <= END_R:
            return n + 7 * (b - FIRST_R - 1)
        n += 7 * (END_R - FIRST_R - 1) + 4
        return n + (b - END_R - 1)
    return 7 * b + (FIRST_R + 3 - 7 * (FIRST_R + 1))


def add_index_of_seq(b):
    late = 3 if not is_int(b) or FIRST_R <= b < END_R else 0
    return adds_before(b + 1) + late


def add_index_of_tile(b, j):
    if j >= 3:
        return adds_before(b + 1) + j - 3
    late = 0 if is_int(b) and b == FIRST_R else 3
    return adds_before(b) + late + 1 + j


class Unit:

    def __init__(self, b, s, end):
        if s < 0:
            b, s = b - 1, s + STEPS
        routing = not is_int(b) or FIRST_R <= b < END_R
        there = not is_int(b) or 0 <= b < end
        self.shared = there and s < 2
        self.routed = there and s >= 2 and routing
        self.there = self.shared or self.routed
        self.tt, self.j, self.b = s, s - 2, b
        self.q = s % 2
        if self.there:
            self.n = units_before(b) + s
        if self.routed:
            self.r = R_PER_SEQ * (b - FIRST_R) + self.j


def build(nc, source, Wq, bq, Wk, bk, Wv, bv, Wc, bc, gate_w, gate_b, w1, b1, w3, b3, w2, b2,
          sw1, sb1, sw3, sb3, sw2, sb2, out):
    B, L, D = source.shape
    assert D == P and L == 2 * P
    KT = L // P
    TILES = B * KT
    TOKENS = TILES * P
    GROUPS = TILES // GROUP
    HT = TILES // HALVES
    RT = 2 * HT + E
    assert RT * HALVES == R_PER_SEQ * (END_R - FIRST_R)
    SCALE = float(DK) ** -0.5
    QCOLS = [L - P * kt for kt in range(KT)]
    QOFF = [sum(QCOLS[:kt]) for kt in range(KT)]
    SW = sum(QCOLS)
    HALF_SEQS = B // HALVES
    SCATTERS = 4
    SCATTERS_LATE = 9
    SCATTER_STEPS = -(-2 * HT // SCATTERS)
    STATS_FIRST = 3
    STATS_PARTS = [slice(0, 2 * GROUP * STATS_FIRST), slice(2 * GROUP * STATS_FIRST, TILES)]
    SMALL, CONSTS = 7, 7
    RT_CHOSEN, RT_COUNTED, RT_STEPS = 25, 37, 52

    x_rows = source.rearrange("b l d -> (b l) d")
    out_rows = out.rearrange("b l d -> (b l) d")
    xnT_dram = nc.dram_tensor("xnT_dram", (B, P, 2 * L), F32).ap()
    xn_dram = nc.dram_tensor("xn_dram", (TOKENS + P, P), F32).ap()
    sum_dram = nc.dram_tensor("sum_dram", (TOKENS + P, P), F32).ap()
    bias_dram = nc.dram_tensor("bias_dram", (NE, 2, 2 * P), F32).ap()
    slots_dram = [nc.dram_tensor(f"slots_dram{h}", (P * RT, 2), I32).ap() for h in range(HALVES)]

    ctx = ExitStack()
    with ctx:
        def sb(name, shape, dt=F32):
            return ctx.enter_context(nc.sbuf_tensor(name, shape, dt))

        def ps(name):
            return ctx.enter_context(nc.psum_tensor(name, [P, 512], F32))

        def sem(name):
            return ctx.enter_context(nc.semaphore(name))

        ident = sb("ident", [P, P])
        mask = sb("mask", [P, L])
        ones2 = sb("ones2", [P, P], F32R)
        before_f = sb("before_f", [P, P])
        before = sb("before", [P, P], F32R)
        ones = sb("ones", [P, P], F32R)
        zeros = sb("zeros", [P, P])
        wqkv = [sb(f"wqkv{part}", [P, 3, H * DK], F32R) for part in range(2)]
        w13 = [sb(f"w13{part}", [P, NE * 4 * P], F32R) for part in range(2)]
        w2T = sb("w2T", [P, NE * P])
        wc = sb("wc", [P, PAIRS, P])
        gateT = [sb(f"gateT{part}", [P, E], F32R) for part in range(2)]
        b13 = sb("b13", [P, NE * 4 * P])
        b2r = sb("b2r", [P, NE * P], F32R)
        bv_bb = sb("bv_bb", [P, H * DK])
        bqk = sb("bqk", [P, 2, PAIRS])
        gate_bb = sb("gate_bb", [P, E])
        out_bias = sb("out_bias", [P, 3, P])
        raw = sb("raw", [P, 4, 1024])
        raw_first = sb("raw_first", [P, 2, P])
        bias13_raw = sb("bias13_raw", [2 * NE, 2 * P])
        bias13 = sb("bias13", [2 * NE, 2 * P])
        bias2 = [sb(f"bias2_{k}", [NE, P], F32R if k else F32) for k in range(3)]
        xs = sb("xs", [P, XS, 2 * GROUP, P])
        stats = sb("stats", [P, XS, 2 * GROUP, 6])
        moments = sb("moments", [P, TILES, 2])
        rstd = sb("rstd", [P, TILES])
        xg = sb("xg", [P, 2, GROUP, P])
        xnT = [sb(f"xnT{part}", [P, 2, GROUP * P], F32R) for part in range(2)]
        logits = sb("logits", [P, TILES, E])
        first_key = sb("first_key", [P, E])
        restart = sb("restart", [P, E, HT])
        tile_no = sb("tile_no", [P, RT])
        token_no = sb("token_no", [P, TILES], I32)
        score = sb("score", [P, HT, E])
        ranked = sb("ranked", [P, HT, E])
        hit = [sb(f"hit{c}", [P, HT, E]) for c in range(2)]
        chosen = sb("chosen", [P, HT, E], F32R)
        scratch = sb("scratch", [P, HT, E])
        count = sb("count", [P, E, HT])
        upto = sb("upto", [P, E, HT])
        red = [sb(f"red{k}", [P, HT]) for k in range(2)]
        weight = [sb(f"weight{c}", [P, HT]) for c in range(2)]
        per_e = [sb(f"per_e{k}", [P, E]) for k in range(4)]
        per_e_i = sb("per_e_i", [P, E], I32)
        end_cmp = raw[:, 3, 0:RT * E].rearrange("p (j e) -> p j e", e=E)
        slot_i = [sb(f"slot_i{k}", [P, HT], I32) for k in range(3)]
        slot_f = [sb(f"slot_f{k}", [P, HT]) for k in range(2)]
        pairs = sb("pairs", [P, HALVES, 2, HT, 2], I32)
        slot_row = sb("slot_row", [P, HALVES, 2, HT], U32)
        tile_e = sb("tile_e", [P, RT])
        tile_expert = sb("tile_expert", [P, HALVES * RT], I32)
        slots = sb("slots", [P, HALVES * RT, 2], I32)
        xT = [sb(f"xT{par}", [P, 2, L], F32R) for par in range(2)]
        yout = [sb(f"yout{par}", [P, KT, P]) for par in range(2)]
        qk = sb("qk", [P, 2, 2, L])
        masked_s = sb("masked_s", [P, 2, 2, SW])
        probs = sb("probs", [P, 2, 2, SW])
        neg_max = sb("neg_max", [P, 2, 2, KT])
        denom = sb("denom", [P, 2, KT, 2])
        rdenom = sb("rdenom", [P, 2, KT, 2])
        vb = sb("vb", [P, KT, 2 * P])
        vs = sb("vs", [P, 2, KT, P])
        headsT = sb("headsT", [P, 2, L])
        slot = sb("slot", [P, R_PER_SEQ, 2], I32)
        xu = sb("xu", [P, 2, P])
        xuT = [sb(f"xuT{part}", [P, 2, P], F32R) for part in range(2)]
        hb = sb("hb", [P, 4 * P])
        hgl = sb("hgl", [P, 2, 2 * P])
        gmin = sb("gmin", [P, 2, P])
        lclip = sb("lclip", [P, 2, P])
        th = sb("th", [P, 2, P])
        tg = sb("tg", [P, 2, P])
        act_a = sb("act_a", [P, 2, P])
        aT = sb("aT", [P, 2, P])
        yu = sb("yu", [P, 2, P])

        p_qk, p_v, p_s0, p_s1, p_o, p_acc, p_h, p_t = [ps(n) for n in
            ("p_qk", "p_v", "p_s0", "p_s1", "p_o", "p_acc", "p_h", "p_t")]
        p_s = [p_s0, p_s1]

        zeroed = sem("zeroed")
        zeroed_dve = sem("zeroed_dve")
        consts = sem("consts")
        bias_raw_in = sem("bias_raw_in")
        bias_hi = sem("bias_hi")
        bias_lo = sem("bias_lo")
        bias_in = sem("bias_in")
        bias_ordered = sem("bias_ordered")
        bias_in_dram = sem("bias_in_dram")
        b13_in = [sem(f"b13_in_{name}") for name in ("shared", "routed")]
        small_in = sem("small_in")
        raw_qkv_in = sem("raw_qkv_in")
        raw_13_in = [sem(f"raw_13_in{i}") for i in range(2)]
        raw_w2_in = sem("raw_w2_in")
        first_raw_in = sem("first_raw_in")
        wT_done = sem("wT_done")
        w2T_done = sem("w2T_done")
        gate_hi = sem("gate_hi")
        w2T_ready = sem("w2T_ready")
        wT_hi = sem("wT_hi")
        wT_lo = sem("wT_lo")
        qkv_hi = sem("qkv_hi")
        weights_ready = sem("weights_ready")
        sum_init = sem("sum_init")
        slots_init = sem("slots_init")
        xs_in = [sem(f"xs_in{i}") for i in range(XS)]
        stats_done = sem("stats_done")
        moments_done = sem("moments_done")
        std_done = sem("std_done")
        rstd_done = sem("rstd_done")
        xg_in = [sem(f"xg_in{i}") for i in range(2)]
        xn_done = [sem(f"xn_done_{name}") for name in ("first", "later")]
        xn_stored = [sem(f"xn_stored{i}") for i in range(2)]
        xnT_done = sem("xnT_done")
        xnT_hi = sem("xnT_hi")
        xnT_lo = sem("xnT_lo")
        xnT_stored = [sem(f"xnT_stored{i}") for i in range(2)]
        gate_done = sem("gate_done")
        logits_ready = sem("logits_ready")
        rt = sem("rt")
        gate_sub = sem("gate_sub")
        gate_exp = sem("gate_exp")
        counted = sem("counted")
        scattered = [sem(f"scattered{h}") for h in range(HALVES)]
        slots_in = [sem(f"slots_in{h}") for h in range(HALVES)]
        first_xT = sem("first_xT")
        xT_in = [sem(f"xT_in{i}") for i in range(2)]
        qk_proj = sem("qk_proj")
        qk_ready = sem("qk_ready")
        scores_done = sem("scores_done")
        masked = sem("masked")
        probs_ready = sem("probs_ready")
        rdenom_done = sem("rdenom_done")
        v_proj = sem("v_proj")
        v_biased = sem("v_biased")
        v_scaled = sem("v_scaled")
        av_done = sem("av_done")
        heads_ready = sem("heads_ready")
        wc_done = sem("wc_done")
        y_ready = sem("y_ready")
        added = sem("added")
        slot_ready = sem("slot_ready")
        xu_in = [sem(f"xu_in{i}") for i in range(2)]
        xuT_done = sem("xuT_done")
        xuT_hi = sem("xuT_hi")
        xuT_lo = sem("xuT_lo")
        h_done = sem("h_done")
        h_biased = sem("h_biased")
        hgl_done = sem("hgl_done")
        g_ready = sem("g_ready")
        l_ready = sem("l_ready")
        tanh_done = sem("tanh_done")
        tg_done = sem("tg_done")
        a_ready = sem("a_ready")
        aT_done = sem("aT_done")
        aT_ready = sem("aT_ready")
        yu_done = sem("yu_done")
        yu_ready = sem("yu_ready")
        out_stored = sem("out_stored")
        waits_apart = sem("waits_apart")

        def apart(eng):
            eng.sem_inc(waits_apart, 1)

        def unit(b, s):
            return Unit(b, s, B)

        def group_at(b, s, late):
            if not is_int(b):
                return None
            k = STEPS * b + s - late
            g = k // 2 + 1
            return g if k >= 0 and k % 2 == 0 and g < GROUPS else None

        def half_at(b, s, late):
            if not is_int(b):
                return None
            for h in range(HALVES):
                if STEPS * b + s == 2 * (GROUPS // HALVES * (h + 1) - 2) + 3 + late:
                    return h
            return None

        def w13_raw(e):
            return raw[:, 3 if e == E else 2 + e % 2, 0:4 * P].rearrange("p (w u d) -> p w u d", w=2, u=2)

        w2_raw = raw[:, 0, :].rearrange("p (e f) -> p e f", e=E)
        sw2_raw, gate_raw = raw_first[:, 0, :], raw_first[0:E, 1, :]

        def stats_at(b, s):
            k = STEPS * b + s if is_int(b) else 0
            return STATS_FIRST + k // 2 if k % 2 and k // 2 < GROUPS // 2 - STATS_FIRST else None

        w13_steps = (3, 4, 6, 11, 12, 14, 19, 20)

        def w13_at(b, s):
            return w13_steps.index(STEPS * b + s) if is_int(b) and STEPS * b + s in w13_steps else None

        def w2_at(b, s):
            return b if is_int(b) and b < E // 4 and s == 2 else None

        weight_of_slot = slot[:, :, 1:2].bitcast(F32)

        def normalise(eng, g):
            eng.wait_ge(rstd_done, 2 if g < 2 * STATS_FIRST else 4)
            eng.wait_ge(xg_in[g % 2], 16 * (g // 2 + 1))
            for t in range(GROUP):
                n = g * GROUP + t
                ins = eng.tensor_scalar(xg[:, g % 2, t, :], xg[:, g % 2, t, :], moments[:, n, 0:1], rstd[:, n:n + 1],
                                        ALU.subtract, ALU.mult)
            ins.then_inc(xn_done[g > 0], 1)

        block = ctx.enter_context(nc.Block())

        def main_loop(eng, sequence):
            for i in range(FIRST_R // 2 + 1):
                for par in range(2):
                    sequence(i, par)
            with eng.Fori(FIRST_R // 2 + 1, END_R // 2) as i:
                for par in range(2):
                    sequence(i, par)
            for i in range(END_R // 2, B // 2):
                for par in range(2):
                    sequence(i, par)

        @block.sync
        def _(sp):
            def load_x(g):
                sp.dma_start(xg[:, g % 2], x_rows[g * GROUP * P:(g + 1) * GROUP * P].rearrange("(t p) d -> p t d", p=P)).then_inc(xg_in[g % 2], 16)

            load_x(0)
            raw13, raw2 = bias13_raw, bias2[0]
            for w, (routed, shared) in enumerate(((b1, sb1), (b3, sb3))):
                sp.dma_start(raw13[w * NE:w * NE + E, :], routed).then_inc(bias_raw_in, 16)
                sp.dma_start(raw13[w * NE + E:w * NE + NE, :], shared.rearrange("(a f) -> a f", a=1)).then_inc(bias_raw_in, 16)
            sp.dma_start(raw2[0:E, :], b2).then_inc(bias_raw_in, 16)
            sp.dma_start(raw2[E:NE, :], sb2.rearrange("(a f) -> a f", a=1)).then_inc(bias_raw_in, 16)
            for i, w in enumerate((Wq, Wk, Wv)):
                sp.dma_start(raw[:, i, :].rearrange("p (h k) -> p h k", h=H), w.rearrange("h d k -> d h k")).then_inc(raw_qkv_in, 16)

            def load_w13(e):
                for w, (routed, shared) in enumerate(((w1, sw1), (w3, sw3))):
                    src = routed[e] if e < E else shared
                    sp.dma_start(w13_raw(e)[:, w], src.rearrange("(u p) d -> p u d", p=P)).then_inc(raw_13_in[1 if e == E else e % 2], 16)

            load_w13(E)
            sp.dma_start(sw2_raw, sw2).then_inc(first_raw_in, 16)
            sp.dma_start(gate_raw, gate_w).then_inc(first_raw_in, 16)
            sp.dma_start(wc[:, :, :], Wc.rearrange("(c p) n -> p c n", p=P)).then_inc(small_in, 16)
            for j, bias in enumerate((bq, bk)):
                sp.dma_start(bqk[:, j, :], bias.rearrange("(c u) k -> (u k) c", u=2), allow_slow_non_contiguous=True).then_inc(small_in, 16)
            sp.dma_start(gate_bb[:, :], gate_b.rearrange("(a e) -> a e", a=1).to_broadcast([P, E])).then_inc(small_in, 16)
            for k, bias in enumerate((bc, sb2)):
                sp.dma_start(out_bias[:, k, :], bias.rearrange("(a e) -> a e", a=1).to_broadcast([P, P])).then_inc(small_in, 16)
            sp.dma_start(bv_bb[:, :], bv.rearrange("h k -> (h k)").rearrange("(a n) -> a n", a=1).to_broadcast([P, H * DK])).then_inc(small_in, 16)
            load_x(1)
            sp.wait_ge(bias_ordered, 1)
            for w in range(2):
                sp.dma_start(bias_dram[:, w, :], bias13[w * NE:(w + 1) * NE, :]).then_inc(bias_in_dram, 16)

            def spread_bias(e0, e1):
                src = bias_dram[e0:e1].rearrange("e w f -> (e w f)").rearrange("(a n) -> a n", a=1)
                sp.dma_start(b13[:, e0 * 4 * P:e1 * 4 * P], src.to_broadcast([P, (e1 - e0) * 4 * P])).then_inc(b13_in[e0 == 0], 16)

            sp.wait_ge(zeroed, 1)
            sp.wait_ge(bias_hi, 1)
            sp.wait_ge(bias_lo, 1)
            for part, row in enumerate((0, 32)):
                sp.dma_start(b2r[row:row + 1, :].bitcast(F32).rearrange("p (e d) -> p e d", e=NE), bias2[1 + part][:, :].bitcast(F32)).then_inc(bias_in, 16)
            sp.wait_ge(bias_in_dram, 32)
            spread_bias(E, NE)
            sp.wait_ge(zeroed_dve, 1)
            sp.dma_start(xn_dram[TOKENS:TOKENS + P, :], zeros[:, :]).then_inc(sum_init, 16)
            sp.dma_start(sum_dram[TOKENS:TOKENS + P, :], zeros[:, :]).then_inc(sum_init, 16)

            def store_xn(g):
                sp.wait_ge(xn_done[g > 0], max(g, 1))
                sp.dma_start(xn_dram[g * GROUP * P:(g + 1) * GROUP * P].rearrange("(t p) d -> p t d", p=P), xg[:, g % 2]).then_inc(xn_stored[g % 2], 16)

            def store_xnT(g):
                sp.wait_ge(xnT_lo, g + 1)
                for part in range(2):
                    n = GROUP // KT
                    dst = xnT_dram[g * n:(g + 1) * n].rearrange("s p (a l) -> p s a l", a=2)[:, :, part]
                    sp.dma_start(dst, xnT[part][:, g % 2].bitcast(F32).rearrange("p (s l) -> p s l", l=L)).then_inc(xnT_stored[g % 2], 16)

            def load_seq(b, par):
                sp.dma_start(xT[par][:, :, :].bitcast(F32).rearrange("p a l -> p (a l)"),
                             xnT_dram[bass.ds(b, 1)].rearrange("s p n -> (s p) n")).then_inc(xT_in[par], 16)

            def copy_out(lo, hi):
                def rows(t):
                    return t[lo:hi].rearrange("(a r) d -> a (r d)", a=P)
                sp.dma_start(rows(out_rows), rows(sum_dram)).then_inc(out_stored, 16)

            def load_slots(h):
                sp.wait_ge(scattered[h], 16 * 2 * HT)
                sp.dma_start(slots[:, h * RT:(h + 1) * RT, :].rearrange("p j c -> p (j c)"),
                             slots_dram[h].rearrange("(p j) c -> p (j c)", p=P)).then_inc(slots_in[h], 16)

            sp.wait_ge(weights_ready, 2)
            load_w13(0)
            sp.dma_start(w2_raw, w2.rearrange("e d f -> d e f")).then_inc(raw_w2_in, 16)
            sp.wait_ge(wT_done, 1)
            load_w13(1)
            store_xn(0)
            store_xnT(0)
            def init_sum(k):
                lo, hi = k * TOKENS // 4, (k + 1) * TOKENS // 4
                sp.dma_start(sum_dram[lo:hi].rearrange("(a r) d -> a (r d)", a=P), x_rows[lo:hi].rearrange("(a r) d -> a (r d)", a=P)).then_inc(sum_init, 16)

            for b in range(FIRST_R):
                for s in range(STEPS):
                    g = group_at(b, s, 0)
                    if g is not None:
                        if g + 1 < GROUPS:
                            sp.wait_ge(xnT_done, g)
                            sp.wait_ge(xn_stored[(g - 1) % 2], 16 * ((g - 1) // 2 + 1))
                            load_x(g + 1)
                        store_xn(g)
                    g = group_at(b, s, 1)
                    if g is not None:
                        store_xnT(g)
                    if STEPS * b + s in range(6, 10):
                        init_sum(STEPS * b + s - 6)
                    if (b, s) == (2, 0):
                        spread_bias(0, E)
                    e = w13_at(b, s)
                    if e is not None and e + 2 < E:
                        sp.wait_ge(wT_done, e + 2)
                        load_w13(e + 2)
                    h = half_at(b, s, SCATTERS_LATE + SCATTER_STEPS)
                    if h is not None:
                        load_slots(h)
                sp.wait_ge(v_proj, PAIRS // 2 * (b + 1))
                g = (b + 2) // (GROUP // KT)
                sp.wait_ge(xnT_stored[g % 2], 32 * (g // 2 + 1))
                load_seq(b + 2, b % 2)

            def reload(i0, i1):
                with sp.Fori(i0, i1) as i:
                    for par in range(2):
                        sp.wait_ge(v_proj, PAIRS // 2 * (2 * i + par + 1))
                        apart(sp)
                        load_seq(2 * i + par + 2, par)

            last = RT - 1
            done_in = FIRST_R + last // R_PER_SEQ
            need = max(add_index_of_tile(done_in, last % R_PER_SEQ), add_index_of_seq(HALF_SEQS - 1)) + 1
            reload(FIRST_R // 2, FIRST_R // 2 + 1)
            load_slots(HALVES - 1)
            reload(FIRST_R // 2 + 1, done_in // 2 + 1)
            sp.wait_ge(added, 16 * need)
            copy_out(0, TOKENS // HALVES)
            reload(done_in // 2 + 1, B // 2 - 1)
            sp.wait_ge(added, 16 * (add_index_of_seq(END_R - 1) + 1))
            copy_out(TOKENS // HALVES, END_R * L)
            sp.wait_ge(added, 16 * (add_index_of_seq(B - 1) + 1))
            copy_out(END_R * L, TOKENS)
            sp.wait_ge(out_stored, 48)

        @block.gpsimd
        def _(pool):
            pool.memset(b2r[:, :].bitcast(F32), 0.0).then_inc(zeroed, 1)
            pool.memset(ident[:, :], 0.0).then_inc(zeroed, 1)
            pool.memset(mask[:, :], 0.0).then_inc(zeroed, 1)
            pool.memset(before_f[:, :], 1.0).then_inc(zeroed, 1)
            pool.wait_ge(zeroed, 4)
            pool.affine_select(out=ident[:, :], in_=ident[:, :], compare_op=ALU.not_equal, fill=1.0, base=0,
                               pattern=[[-1, P]], channel_multiplier=1).then_inc(consts, 1)
            pool.affine_select(out=mask[:, 0:P], in_=mask[:, 0:P], compare_op=ALU.is_ge, fill=MASKED, base=0,
                               pattern=[[1, P]], channel_multiplier=-1).then_inc(consts, 1)
            pool.affine_select(out=before_f[:, :], in_=before_f[:, :], compare_op=ALU.is_ge, fill=0.0,
                               base=-1, pattern=[[1, P]], channel_multiplier=-1).then_inc(consts, 1)
            pool.iota(token_no[:, :], [[P, TILES]], base=0, channel_multiplier=1).then_inc(consts, 1)
            pool.iota(tile_no[:, :], [[1, RT]], base=0, channel_multiplier=0,
                      allow_small_or_imprecise_dtypes=True).then_inc(consts, 1)
            empty = slots[:, 0:RT, :]
            pool.iota(empty[:, :, 0], [[0, RT]], base=TOKENS, channel_multiplier=1).then_inc(consts, 1)
            pool.memset(empty[:, :, 1], 0).then_inc(consts, 1)
            pool.wait_ge(consts, CONSTS)
            for h in range(HALVES):
                pool.dma_start(slots_dram[h].rearrange("(p j) c -> p (j c)", p=P), empty.rearrange("p j c -> p (j c)")).then_inc(slots_init, 16)

            def scatter_slots(h, part, first):
                if part == 0:
                    pool.wait_ge(slots_init, 16 * HALVES)
                    pool.wait_ge(rt, RT_STEPS * (h + 1))
                late = max(part - first, 0)
                n0 = (part - late) * SCATTERS + late * SCATTERS // 2
                n1 = n0 + (SCATTERS // 2 if part >= first else SCATTERS)
                for n in range(n0, min(n1, 2 * HT)):
                    c, t = divmod(n, HT)
                    pool.indirect_dma_start(
                        out=slots_dram[h][:, :], out_offset=bass.IndirectOffsetOnAxis(ap=slot_row[:, h, c, t:t + 1], axis=0),
                        in_=pairs[:, h, c, t, :], in_offset=None).then_inc(scattered[h], 16)

            def gather(u):
                if is_int(u.r) and u.r in (0, RT):
                    pool.wait_ge(slots_in[u.r // RT], 16)
                if not is_int(u.r) and u.j == 0:
                    pool.wait_ge(slots_in[HALVES - 1], 16)
                if not is_int(u.r) or u.r >= R_PER_SEQ:
                    pool.wait_ge(added, 16 * (add_index_of_tile(u.b - 1, u.j) + 1))
                pool.tensor_copy(slot[:, u.j, :], slots[:, bass.ds(u.r, 1), :].rearrange("p a c -> p (a c)")).then_inc(slot_ready, 1)
                if not is_int(u.r) or u.r >= 2:
                    pool.wait_ge(xuT_done, u.r - 1)
                    apart(pool)
                pool.wait_ge(slot_ready, u.r + 1)
                apart(pool)
                pool.indirect_dma_start(out=xu[:, u.j % 2, :], out_offset=None, in_=xn_dram[:, :],
                                        in_offset=bass.IndirectOffsetOnAxis(ap=slot[:, u.j, 0:1].bitcast(U32), axis=0)).then_inc(xu_in[u.j % 2], 16)

            def before_add(n):
                if is_int(n) and n == 0:
                    pool.wait_ge(sum_init, 16 * 6)
                else:
                    pool.wait_ge(added, 16 * n)
                    apart(pool)

            def add_tile(u):
                pool.wait_ge(yu_ready, u.r + 1)
                apart(pool)
                before_add(add_index_of_tile(u.b, u.j))
                pool.indirect_dma_start(out=sum_dram[:, :], out_offset=bass.IndirectOffsetOnAxis(ap=slot[:, u.j, 0:1].bitcast(U32), axis=0),
                                        in_=yu[:, u.q, :], in_offset=None, compute_op=ALU.add).then_inc(added, 16)

            def add_seq(b, par):
                pool.wait_ge(y_ready, b + 1)
                apart(pool)
                before_add(add_index_of_seq(b))
                pool.dma_start(sum_dram[bass.ds(b * L, L)].rearrange("(t p) d -> p t d", p=P), yout[par][:, :, :],
                               accum_op=ALU.add).then_inc(added, 16)

            def sequence(i, par):
                b = 2 * i + par
                for s in range(STEPS):
                    g = group_at(b, s, 0)
                    if g is not None:
                        normalise(pool, g)
                    nxt = unit(b, s + 2)
                    if s + 2 < STEPS and nxt.routed:
                        gather(nxt)
                    u = unit(b, s - 3)
                    if u.routed:
                        add_tile(u)
                    if s == 3 and not (is_int(b) and b == 0):
                        add_seq(b - 1, 1 - par)
                    for part in range(2 * SCATTER_STEPS):
                        h = half_at(b, s, SCATTERS_LATE + part)
                        if h is not None:
                            scatter_slots(h, part, STEPS * (FIRST_R - b) - s + part)

            main_loop(pool, sequence)
            add_seq(B - 1, 1)

        @block.scalar
        def _(act):
            def load_stats(g):
                if g >= XS:
                    act.wait_ge(stats_done, g - XS + 1)
                act.dma_start(xs[:, g % XS], x_rows[g * 2 * GROUP * P:(g + 1) * 2 * GROUP * P].rearrange("(t p) d -> p t d", p=P)).then_inc(xs_in[g % XS], 16)

            def split_w13(e, bank):
                act.wait_ge(wT_done, 1 if e == E else e + 2)
                for w in range(2):
                    ins = act.activation(w13[0][:, (4 * e + 2 * w) * P:(4 * e + 2 * w + 2) * P].rearrange("p (two j) -> p two j", two=2),
                                         bank[:, 2 * P * w:2 * P * (w + 1)].rearrange("p (j two) -> p two j", two=2), ACT.Copy)
                ins.then_inc(wT_hi, 1)

            def halve_w2(e, n, bank, k):
                act.wait_ge(w2T_done, k)
                act.activation(w2T[:, e * P:(e + n) * P], bank[:, 0:n * P], ACT.Copy, scale=0.5).then_inc(w2T_ready, 1)

            def take_root(part):
                act.wait_ge(moments_done, part + 1)
                cols = STATS_PARTS[part]
                act.activation(rstd[:, cols], rstd[:, cols], ACT.Sqrt).then_inc(std_done, 1)

            for g in range(XS + STATS_FIRST):
                load_stats(g)
            take_root(0)
            act.wait_ge(raw_qkv_in, 48)
            for i in range(3):
                act.activation(wqkv[0][:, i, :], raw[:, i, :], ACT.Copy).then_inc(qkv_hi, 1)
            split_w13(E, p_s[0])
            halve_w2(E, 1, p_h, 1)
            act.activation(gateT[0][:, :], p_h[:, P:P + E], ACT.Copy).then_inc(gate_hi, 1)

            def split_xnT(g):
                act.wait_ge(xnT_done, g + 1)
                if g >= 2:
                    act.wait_ge(xnT_stored[g % 2], 32 * (g // 2))
                act.activation(xnT[0][:, g % 2, :], p_t[:, :], ACT.Copy).then_inc(xnT_hi, 1)

            def copy_logits(g):
                act.wait_ge(gate_done, g + 1)
                act.activation(logits[:, g * GROUP:(g + 1) * GROUP, :].rearrange("p t e -> p (t e)"), p_t[:, 0:GROUP * E],
                               ACT.Copy).then_inc(logits_ready, 1)

            def qk_evac(b, p):
                act.wait_ge(qk_proj, PAIRS * b + p + 1)
                for j in range(2):
                    ins = act.activation(qk[:, p % 2, j, :], p_qk[:, j * L:(j + 1) * L], ACT.Identity, bias=bqk[:, j, p:p + 1])
                ins.then_inc(qk_ready, 1)

            def exps(b, p, hh):
                if hh == 0 and not (is_int(b) and b == 0 and p < 2):
                    act.wait_ge(av_done, PAIRS * b + p - 1)
                act.wait_ge(masked, 2 * (PAIRS * b + p) + hh + 1)
                for kt in range(KT):
                    cols = slice(QOFF[kt], QOFF[kt] + QCOLS[kt])
                    ins = act.activation(probs[:, p % 2, hh, cols], masked_s[:, p % 2, hh, cols], ACT.Exp,
                                         bias=neg_max[:, p % 2, hh, kt:kt + 1], scale=-1.0,
                                         accum_out=denom[:, p % 2, kt, hh:hh + 1])
                ins.then_inc(probs_ready, 1)

            def heads_evac(b, p):
                act.wait_ge(av_done, PAIRS * b + p + 1)
                if not (is_int(b) and b == 0 and p < 2):
                    act.wait_ge(wc_done, PAIRS * b + p - 1)
                act.activation(headsT[:, p % 2, :], p_o[:, 0:L], ACT.Copy).then_inc(heads_ready, 1)

            def split_xu(u):
                act.wait_ge(xuT_done, u.r + 1)
                act.activation(xuT[0][:, u.q, :], p_o[:, L:L + P], ACT.Copy).then_inc(xuT_hi, 1)

            def tanh(u):
                act.wait_ge(g_ready, u.n + 1)
                act.activation(th[:, u.q, :], gmin[:, u.q, :], ACT.Tanh, scale=ALPHA / 2).then_inc(tanh_done, 1)

            def evac_aT(u):
                act.wait_ge(aT_done, u.n + 1)
                act.activation(aT[:, u.q, :], p_t[:, P:2 * P], ACT.Copy).then_inc(aT_ready, 1)

            def weigh(u):
                act.wait_ge(yu_done, u.r + 1)
                if not is_int(u.r) or u.r >= 2:
                    b, j = (u.b, u.j - 2) if u.j >= 2 else (u.b - 1, u.j + R_PER_SEQ - 2)
                    act.wait_ge(added, 16 * (add_index_of_tile(b, j) + 1))
                act.activation(yu[:, u.q, :], p_t[:, 2 * P:3 * P], ACT.Copy, scale=weight_of_slot[:, u.j, :]).then_inc(yu_ready, 1)

            def sequence(i, par):
                b = 2 * i + par
                for s in range(STEPS):
                    if s + 1 < PAIRS:
                        qk_evac(b, s + 1)
                    elif not (is_int(b) and b == B - 1):
                        qk_evac(b + 1, 0)
                    exps(b, s, 0)
                    if unit(b, s - 1).there:
                        evac_aT(unit(b, s - 1))
                    if not (is_int(b) and b == 0 and s == 0):
                        heads_evac(*((b, s - 1) if s else (b - 1, PAIRS - 1)))
                    if w13_at(b, s) is not None:
                        split_w13(w13_at(b, s), p_h)
                    if w2_at(b, s) is not None:
                        halve_w2(4 * w2_at(b, s), 4, p_h, w2_at(b, s) + 2)
                    exps(b, s, 1)
                    if unit(b, s).there:
                        tanh(unit(b, s))
                    u = unit(b, s + 1)
                    if s + 1 < STEPS and u.routed:
                        split_xu(u)
                    if unit(b, s - 2).routed:
                        weigh(unit(b, s - 2))
                    g = group_at(b, s, 1)
                    if g is not None:
                        split_xnT(g)
                    g = group_at(b, s, 2)
                    if g is not None:
                        copy_logits(g)
                    g = stats_at(b, s)
                    if g is not None and g + XS < GROUPS // 2:
                        load_stats(g + XS)
                    if g == GROUPS // 2 - 1:
                        take_root(1)
                    h = half_at(b, s, 2)
                    if h is not None:
                        act.wait_ge(gate_sub, h + 1)
                        act.activation(score[:, :, :], score[:, :, :], ACT.Exp).then_inc(gate_exp, 1)

            split_xnT(0)
            act.wait_ge(xnT_hi, 1)
            for par in range(2):
                act.activation(xT[par][:, 0, :], xnT[0][:, 0, par * L:(par + 1) * L].bitcast(F32), ACT.Copy).then_inc(first_xT, 1)
            act.wait_ge(small_in, 16 * SMALL)
            qk_evac(0, 0)
            copy_logits(0)
            main_loop(act, sequence)
            heads_evac(B - 1, PAIRS - 1)

        @block.tensor
        def _(pe):
            def three(dst, stat, mov, start, stop, **kw):
                pe.matmul(dst, stat[0], mov[0], start=start, stop=False, **kw)
                pe.matmul(dst, stat[1], mov[0], start=False, stop=False, **kw)
                return pe.matmul(dst, stat[0], mov[1], start=False, stop=stop, **kw)

            def turn_w13(e, bank):
                if e < E:
                    pe.wait_ge(wT_lo, e + 1)
                pe.wait_ge(raw_13_in[1 if e == E else e % 2], 32 if e == E else 32 * (e // 2 + 1 + e % 2))
                for w in range(2):
                    for u in range(2):
                        ins = pe.transpose(bank[:, (2 * w + u) * P:(2 * w + u + 1) * P], w13_raw(e)[:, w, u, :], ident[:, :])
                ins.then_inc(wT_done, 1)

            def turn_w2(k):
                pe.wait_ge(raw_w2_in, 16)
                for e in range(4):
                    ins = pe.transpose(p_h[:, e * P:(e + 1) * P], w2_raw[:, 4 * k + e, :], ident[:, :])
                ins.then_inc(w2T_done, 1)

            pe.wait_ge(consts, 3)
            turn_w13(E, p_s[0])
            pe.wait_ge(first_raw_in, 32)
            pe.transpose(p_h[:, 0:P], sw2_raw, ident[:, :])
            pe.transpose(p_h[:, P:P + E], gate_raw, ident[0:E, 0:E]).then_inc(w2T_done, 1)

            def wait_turned(b, s):
                if STEPS * b + s >= 1:
                    pe.wait_ge(aT_ready, units_before(b) + min(s, 2))

            def turn_xn(g, b, s):
                pe.wait_ge(xn_done[g > 0], max(g, 1))
                if g >= 1:
                    pe.wait_ge(logits_ready, g)
                wait_turned(b, s)
                for t in range(GROUP):
                    ins = pe.transpose(p_t[:, t * P:(t + 1) * P], xg[:, g % 2, t, :], ident[:, :])
                ins.then_inc(xnT_done, 1)

            def gate(g, b, s):
                pe.wait_ge(xnT_lo, g + 1)
                wait_turned(b, s)
                for t in range(GROUP):
                    cols = slice(t * P, (t + 1) * P)
                    ins = three(p_t[:, t * E:(t + 1) * E], [xnT[k][:, g % 2, cols] for k in range(2)],
                                [gateT[k][:, :] for k in range(2)], start=True, stop=True, skip_group_check=True)
                ins.then_inc(gate_done, 1)

            def count_tokens(h, b):
                pe.wait_ge(h_biased, units_before(b + 1))
                pe.wait_ge(wT_lo, NE)
                pe.wait_ge(rt, RT_STEPS * h + RT_CHOSEN)
                m = chosen[:, :, :].rearrange("p t e -> p (t e)")
                pe.matmul(p_h[:, 0:HT * E], before[:, :], m, start=True, stop=True, skip_group_check=True)
                pe.matmul(p_h[:, HT * E:2 * HT * E], ones[:, :], m, start=True, stop=True, skip_group_check=True).then_inc(counted, 1)

            def turn_xu(u, b, s):
                pe.wait_ge(xu_in[u.j % 2], 16 * ((u.r - u.j % 2) // 2 + 1) if is_int(u.r) else 8 * (u.r - u.j % 2) + 16)
                pe.wait_ge(heads_ready, PAIRS * b + s)
                pe.transpose(p_o[:, L:L + P], xu[:, u.j % 2, :], ident[:, :]).then_inc(xuT_done, 1)

            def unit_in(u, par):
                if not (is_int(u.n) and u.n == 0):
                    pe.wait_ge(h_biased, u.n)
                if u.tt == 0 and is_int(u.b) and 0 < u.b <= 3:
                    pe.wait_ge(wT_lo, sum(k < STEPS * u.b for k in w13_steps) + 1)
                for h in range(HALVES):
                    if u.tt == 0 and is_int(u.b) and h in [half_at(u.b - 1, s, 6) for s in range(2, STEPS)]:
                        pe.wait_ge(rt, RT_STEPS * h + RT_COUNTED)
                if u.shared:
                    stat = [xT[par][:, k, u.tt * P:(u.tt + 1) * P] for k in range(2)]
                    w = [w[:, E * 4 * P:] for w in w13]
                else:
                    pe.wait_ge(xuT_lo, u.r + 1)
                    stat = [xuT[k][:, u.q, :] for k in range(2)]
                    at = bass.ds(expert[u.j] * (4 * P), 4 * P)
                    w = [w[:, at] for w in w13]
                three(p_h[:, :], stat, w, start=True, stop=True).then_inc(h_done, 1)

            def unit_turn(u, b, s):
                pe.wait_ge(a_ready, u.n + 1)
                g = group_at(b, s, 2)
                if g is not None:
                    pe.wait_ge(xnT_lo, g + 1)
                g = group_at(b, s, 3)
                if g is not None:
                    pe.wait_ge(logits_ready, g + 1)
                if unit(b, s - 3).routed:
                    pe.wait_ge(yu_ready, unit(b, s - 3).r + 1)
                pe.transpose(p_t[:, P:2 * P], act_a[:, u.q, :], ident[:, :]).then_inc(aT_done, 1)

            def unit_out(u, b, s):
                pe.wait_ge(aT_ready, u.n + 1)
                nxt = unit(b, s - 1)
                if nxt.there:
                    pe.wait_ge(aT_ready, nxt.n + 1)
                if u.shared:
                    pe.matmul(p_acc[:, u.tt * P:(u.tt + 1) * P], aT[:, u.q, :], w2T[:, E * P:], start=False, stop=False,
                              skip_group_check=True)
                else:
                    at = bass.ds(expert[u.j] * P, P)
                    dst = p_t[:, 2 * P:3 * P]
                    pe.matmul(dst, aT[:, u.q, :], w2T[:, at], start=True, stop=False, skip_group_check=True)
                    pe.matmul(dst, ones2[:, :], b2r[:, at], start=False, stop=True, skip_group_check=True).then_inc(yu_done, 1)

            def project_qk(b, p, par):
                if p == 0:
                    if is_int(b) and b < 2:
                        pe.wait_ge(first_xT, 4)
                    else:
                        pe.wait_ge(xT_in[par], 16 * ((b - par) // 2) if is_int(b) else 8 * (b - par))
                if not (is_int(b) and b == 0 and p == 0):
                    pe.wait_ge(qk_ready, PAIRS * b + p)
                for j in range(2):
                    ins = three(p_qk[:, j * L:(j + 1) * L], [w[:, j, p * P:(p + 1) * P] for w in wqkv],
                                [xT[par][:, k, :] for k in range(2)], start=True, stop=True)
                ins.then_inc(qk_proj, 1)

            def scores(b, p):
                pe.wait_ge(qk_ready, PAIRS * b + p + 1)
                if not (is_int(b) and b == 0 and p == 0):
                    pe.wait_ge(masked, 2 * (PAIRS * b + p))
                for kt in range(KT):
                    for hh in range(2):
                        rows = slice(DK * hh, DK * (hh + 1))
                        ins = pe.matmul(p_s[hh][:, QOFF[kt]:QOFF[kt] + QCOLS[kt]],
                                        qk[rows, p % 2, 1, kt * P:(kt + 1) * P], qk[rows, p % 2, 0, kt * P:L],
                                        start=True, stop=True, skip_group_check=True)
                        if kt == KT - 1:
                            ins.then_inc(scores_done, 1)

            def project_v(b, g, par):
                if not (is_int(b) and b == 0 and g == 0):
                    pe.wait_ge(v_biased, PAIRS // 2 * b + g)
                cols = slice(g * 2 * P, (g + 1) * 2 * P)
                for kt in range(KT):
                    dst = p_v[:, kt * 2 * P:(kt + 1) * 2 * P]
                    ins = three(dst, [xT[par][:, k, kt * P:(kt + 1) * P] for k in range(2)],
                                [w[:, 2, cols] for w in wqkv], start=True, stop=True)
                ins.then_inc(v_proj, 1)

            def values(b, p, turned):
                pe.wait_ge(v_scaled, PAIRS * b + p + 1)
                if turned and turned.routed:
                    pe.wait_ge(xuT_lo, turned.r + 1)
                if not (is_int(b) and b == 0 and p == 0):
                    pe.wait_ge(heads_ready, PAIRS * b + p)
                for kt in range(KT):
                    for hh in range(2):
                        rows = slice(DK * hh, DK * (hh + 1))
                        ins = pe.matmul(p_o[rows, kt * P:L], vs[:, p % 2, kt, rows],
                                        probs[:, p % 2, hh, QOFF[kt]:QOFF[kt] + QCOLS[kt]],
                                        start=(kt == 0), stop=(kt == KT - 1), skip_group_check=True)
                ins.then_inc(av_done, 1)

            def out_projection(b, p):
                pe.wait_ge(heads_ready, PAIRS * b + p + 1)
                if p == 0 and not (is_int(b) and b == 0):
                    pe.wait_ge(y_ready, b)
                for tt in range(KT):
                    ins = pe.matmul(p_acc[:, tt * P:(tt + 1) * P], headsT[:, p % 2, tt * P:(tt + 1) * P], wc[:, p, :],
                                    start=(p == 0 and tt == 0), stop=False, skip_group_check=True)
                ins.then_inc(wc_done, 1)

            def pair_before(b, s, late):
                if s >= late:
                    return b, s - late
                return None if is_int(b) and b == 0 else (b - 1, s - late + PAIRS)

            expert = [None] * R_PER_SEQ

            def load_expert(r, j):
                expert[j] = pe.value_load(tile_expert[0:1, bass.ds(r, 1)], min_val=0, max_val=E - 1)

            def sequence(i, par):
                b = 2 * i + par
                r0 = R_PER_SEQ * (b - FIRST_R)
                for s in range(STEPS):
                    scores(b, s)
                    h = half_at(b, s, 6)
                    if h is not None:
                        count_tokens(h, b)
                    u, out_u, nxt = unit(b, s), unit(b, s - 2), unit(b, s + 1)
                    if s + 1 == STEPS or not nxt.routed:
                        nxt = None
                    if u.routed:
                        if is_int(u.r) and u.r % RT == 0:
                            pe.wait_ge(rt, RT_STEPS * (u.r // RT + 1))
                        load_expert(u.r, u.j)
                    if out_u.routed and s < 2:
                        load_expert(out_u.r, out_u.j)
                    if pair_before(b, s, 1):
                        values(*pair_before(b, s, 1), u)
                    if unit(b, s - 1).there:
                        unit_turn(unit(b, s - 1), b, s)
                    if u.there:
                        unit_in(u, par)
                    if w2_at(b, s) is not None:
                        pe.wait_ge(h_biased, units_before(b + 1))
                        turn_w2(w2_at(b, s))
                    if w13_at(b, s) is not None:
                        pe.wait_ge(w2T_ready, min(b, 1) + 2)
                        turn_w13(w13_at(b, s), p_h)
                    if s + 2 < PAIRS:
                        project_qk(b, s + 2, par)
                    elif not (is_int(b) and b == B - 1):
                        project_qk(b + 1, s + 2 - PAIRS, 1 - par)
                    if s % 2 and s + 1 < STEPS:
                        project_v(b, (s + 1) // 2, par)
                    elif s % 2 and not (is_int(b) and b == B - 1):
                        project_v(b + 1, 0, 1 - par)
                    if pair_before(b, s, 2):
                        out_projection(*pair_before(b, s, 2))
                    if nxt:
                        turn_xu(nxt, b, s)
                    if out_u.there:
                        unit_out(out_u, b, s)
                    g = group_at(b, s, 1)
                    if g is not None:
                        turn_xn(g, b, s)
                    g = group_at(b, s, 2)
                    if g is not None:
                        gate(g, b, s)

            turn_xn(0, 0, 0)
            pe.wait_ge(weights_ready, 2)
            project_qk(0, 0, 0)
            project_v(0, 0, 0)
            project_qk(0, 1, 0)
            pe.wait_ge(weights_ready, 3)
            gate(0, 0, 0)
            pe.wait_ge(bias_in, 16 * 2)
            pe.wait_ge(small_in, 16 * SMALL)
            main_loop(pe, sequence)
            out_projection(B - 1, PAIRS - 2)
            values(B - 1, PAIRS - 1, None)
            out_projection(B - 1, PAIRS - 1)

        @block.vector
        def _(dve):
            dve.memset(zeros[:, :], 0.0).then_inc(zeroed_dve, 1)
            dve.memset(ones2[:, :].bitcast(F32), 0.0).then_inc(zeroed_dve, 1)
            dve.wait_ge(zeroed_dve, 2)
            for row in (0, 32):
                dve.memset(ones2[row:row + 1, :].bitcast(F32), 1.0)
            dve.memset(ones[:, :].bitcast(F32), 1.0)
            for e in range(E):
                dve.memset(first_key[:, e:e + 1], float(E - e))
            dve.memset(restart[:, :, 1:], 1.0)
            dve.memset(restart[:, :, 0:1], 0.0).then_inc(weights_ready, 1)
            dve.wait_ge(bias_raw_in, 16 * 6)

            dve.tensor_copy(bias13[:, :].rearrange("p (two j) -> p two j", two=2),
                            bias13_raw[:, :].rearrange("p (j two) -> p two j", two=2)).then_inc(bias_ordered, 1)
            dve.tensor_copy(bias2[1][:, :], bias2[0][:, :]).then_inc(bias_hi, 1)
            dve.wait_ge(bias_hi, 1)
            dve.tensor_tensor(bias2[2][:, :], bias2[0][:, :], bias2[1][:, :].bitcast(F32), ALU.subtract).then_inc(bias_lo, 1)
            dve.wait_ge(consts, 3)
            dve.tensor_copy(before[:, :], before_f[:, :])

            def statistics(g):
                dve.wait_ge(xs_in[g % XS], 16 * (g // XS + 1))
                for t in range(2 * GROUP):
                    ins = dve.bn_stats(stats[:, g % XS, t, :], xs[:, g % XS, t, :])
                ins.then_inc(stats_done, 1)
                dve.wait_ge(stats_done, g + 1)
                for t in range(2 * GROUP):
                    ins = dve.bn_aggr(moments[:, 2 * GROUP * g + t, :], stats[:, g % XS, t, :])
                return ins

            def add_eps(part):
                dve.wait_ge(rstd_done, 2 * part + 1)
                cols = STATS_PARTS[part]
                dve.tensor_scalar(rstd[:, cols], moments[:, cols, 1], EPS, None, ALU.add).then_inc(moments_done, 1)

            def invert_std(part):
                dve.wait_ge(std_done, part + 1)
                cols = STATS_PARTS[part]
                dve.reciprocal(rstd[:, cols], rstd[:, cols]).then_inc(rstd_done, 1)
                dve.wait_ge(rstd_done, 2 * part + 2)

            def split_w13(e, bank):
                dve.wait_ge(wT_hi, 1 if e == E else e + 2)
                for w in range(2):
                    def halves(t):
                        return t[:, (4 * e + 2 * w) * P:(4 * e + 2 * w + 2) * P].rearrange("p (two j) -> p two j", two=2)
                    ins = dve.tensor_tensor(halves(w13[1]), bank[:, 2 * P * w:2 * P * (w + 1)].rearrange("p (j two) -> p two j", two=2),
                                            halves(w13[0]).bitcast(F32), ALU.subtract)
                ins.then_inc(wT_lo, 1)

            for g in range(STATS_FIRST):
                ins = statistics(g)
            ins.then_inc(rstd_done, 1)
            add_eps(0)
            invert_std(0)
            normalise(dve, 0)
            for i in range(3):
                dve.wait_ge(qkv_hi, i + 1)
                ins = dve.tensor_tensor(wqkv[1][:, i, :], raw[:, i, :], wqkv[0][:, i, :].bitcast(F32), ALU.subtract)
            ins.then_inc(weights_ready, 1)

            def split_xnT(g):
                dve.wait_ge(xnT_hi, g + 1)
                if g >= 2:
                    dve.wait_ge(xnT_stored[g % 2], 32 * (g // 2))
                dve.tensor_tensor(xnT[1][:, g % 2, :], p_t[:, :], xnT[0][:, g % 2, :].bitcast(F32), ALU.subtract).then_inc(xnT_lo, 1)

            k = [0]

            def then(ins):
                k[0] += 1
                ins.then_inc(rt, 1)
                dve.wait_ge(rt, k[0])

            def over_experts(t):
                return t[:, :].unsqueeze(2).to_broadcast([P, HT, E])

            def subtract_max(h):
                lg = logits[:, h * HT:(h + 1) * HT, :]
                dve.wait_ge(logits_ready, GROUPS // HALVES * (h + 1))
                then(dve.tensor_reduce(red[0][:, :], lg, AX.X, ALU.max))
                dve.tensor_tensor(score[:, :, :], lg, over_experts(red[0]), ALU.subtract).then_inc(gate_sub, 1)

            def gate_softmax(h):
                dve.wait_ge(consts, CONSTS)
                dve.wait_ge(gate_exp, h + 1)
                then(dve.tensor_reduce(red[0][:, :], score[:, :, :], AX.X, ALU.add))
                then(dve.reciprocal(red[1][:, :], red[0][:, :]))
                then(dve.tensor_tensor(score[:, :, :], score[:, :, :], over_experts(red[1]), ALU.mult))
                then(dve.tensor_tensor(ranked[:, :, :], score[:, :, :], gate_bb[:, :].unsqueeze(1).to_broadcast([P, HT, E]), ALU.add))

            def choose(h, c):
                keys = first_key[:, :].unsqueeze(1).to_broadcast([P, HT, E])
                then(dve.tensor_reduce(red[0][:, :], ranked[:, :, :], AX.X, ALU.max))
                then(dve.tensor_tensor(scratch[:, :, :], ranked[:, :, :], over_experts(red[0]), ALU.is_equal))
                then(dve.tensor_tensor(scratch[:, :, :], scratch[:, :, :], keys, ALU.mult))
                then(dve.tensor_reduce(red[0][:, :], scratch[:, :, :], AX.X, ALU.max))
                then(dve.tensor_tensor(hit[c][:, :, :], keys, over_experts(red[0]), ALU.is_equal))
                if c == 0:
                    then(dve.scalar_tensor_tensor(out=ranked[:, :, :], in0=hit[0][:, :, :], scalar=MASKED, in1=ranked[:, :, :],
                                                  op0=ALU.mult, op1=ALU.add))
                then(dve.tensor_tensor(scratch[:, :, :], hit[c][:, :, :], score[:, :, :], ALU.mult))
                then(dve.tensor_reduce(weight[c][:, :], scratch[:, :, :], AX.X, ALU.add))
                then(dve.tensor_copy(pairs[:, h, c, :, 1].bitcast(F32), weight[c][:, :]))
                then(dve.tensor_copy(pairs[:, h, c, :, 0], token_no[:, h * HT:(h + 1) * HT]))

            def choose_first(h):
                choose(h, 0)

            def choose_second(h):
                choose(h, 1)
                then(dve.tensor_tensor(chosen[:, :, :], hit[0][:, :, :], hit[1][:, :, :], ALU.add))
                assert k[0] == RT_STEPS * h + RT_CHOSEN, k[0]

            def place(h):
                dve.wait_ge(counted, h + 1)
                then(dve.tensor_copy(count[:, :, :], p_h[:, HT * E:2 * HT * E].rearrange("p (t e) -> p e t", e=E)))
                then(dve.tensor_tensor_scan(upto[:, :, :].rearrange("p e t -> p (e t)"), restart[:, :, :].rearrange("p e t -> p (e t)"),
                                            count[:, :, :].rearrange("p e t -> p (e t)"), 0.0, ALU.mult, ALU.add))
                then(dve.tensor_scalar(per_e_i[:, :], upto[:, :, HT - 1], float(P - 1), None, ALU.add))
                then(dve.tensor_single_scalar(per_e_i[:, :], per_e_i[:, :], 7, ALU.arith_shift_right))
                then(dve.tensor_copy(per_e[0][:, :], per_e_i[:, :]))
                then(dve.memset(per_e[1][:, :], 1.0))
                then(dve.tensor_tensor_scan(per_e[2][:, :], per_e[1][:, :], per_e[0][:, :], 0.0, ALU.mult, ALU.add))
                then(dve.tensor_tensor(per_e[3][:, :], per_e[2][:, :], per_e[0][:, :], ALU.subtract))
                then(dve.tensor_scalar(per_e[3][:, :], per_e[3][:, :], float(P), None, ALU.mult))
                then(dve.tensor_tensor(upto[:, :, :], upto[:, :, :], count[:, :, :], ALU.subtract))
                then(dve.tensor_tensor(upto[:, :, :], upto[:, :, :], per_e[3][:, :].unsqueeze(2).to_broadcast([P, E, HT]), ALU.add))
                then(dve.tensor_tensor(ranked[:, :, :], p_h[:, 0:HT * E].rearrange("p (t e) -> p t e", e=E),
                                       upto[:, :, :].rearrange("p e t -> p t e"), ALU.add))
                assert k[0] == RT_STEPS * h + RT_COUNTED, k[0]

            def place_choice(h, c):
                then(dve.tensor_tensor(scratch[:, :, :], hit[c][:, :, :], ranked[:, :, :], ALU.mult))
                then(dve.tensor_reduce(slot_f[0][:, :], scratch[:, :, :], AX.X, ALU.add))
                then(dve.tensor_copy(slot_i[0][:, :], slot_f[0][:, :]))
                then(dve.tensor_single_scalar(slot_i[1][:, :], slot_i[0][:, :], P - 1, ALU.bitwise_and))
                then(dve.tensor_single_scalar(slot_i[2][:, :], slot_i[0][:, :], 7, ALU.arith_shift_right))
                then(dve.scalar_tensor_tensor(out=slot_row[:, h, c, :], in0=slot_i[1][:, :], scalar=float(RT), in1=slot_i[2][:, :],
                                              op0=ALU.mult, op1=ALU.add))

            def place_first(h):
                place_choice(h, 0)

            def place_second(h):
                place_choice(h, 1)
                then(dve.tensor_tensor(end_cmp[:, :, :], tile_no[:, :].unsqueeze(2).to_broadcast([P, RT, E]),
                                       per_e[2][:, :].unsqueeze(1).to_broadcast([P, RT, E]), ALU.is_ge))
                then(dve.tensor_reduce(tile_e[:, :], end_cmp[:, :, :], AX.X, ALU.add))
                then(dve.tensor_scalar(tile_expert[:, h * RT:(h + 1) * RT], tile_e[:, :], float(E - 1), None, ALU.min))
                assert k[0] == RT_STEPS * (h + 1), k[0]

            routing_stages = (None, subtract_max, None, gate_softmax, choose_first, choose_second, place, place_first, place_second)

            def mask_and_max(b, p):
                for hh in range(2):
                    if hh == 0 and not (is_int(b) and b == 0 and p < 2):
                        dve.wait_ge(probs_ready, 2 * (PAIRS * b + p - 1))
                        apart(dve)
                    dve.wait_ge(scores_done, 2 * (PAIRS * b + p) + hh + 1)
                    apart(dve)
                    for kt in range(KT):
                        cols = slice(QOFF[kt], QOFF[kt] + QCOLS[kt])
                        ins = dve.tensor_tensor_reduce(out=masked_s[:, p % 2, hh, cols], in0=p_s[hh][:, cols],
                                                       in1=mask[:, 0:QCOLS[kt]], scale=-SCALE, scalar=-MASKED,
                                                       op0=ALU.add, op1=ALU.min, accum_out=neg_max[:, p % 2, hh, kt:kt + 1])
                    ins.then_inc(masked, 1)

            def bias_values(b, g):
                if not (is_int(b) and b == 0 and g == 0):
                    dve.wait_ge(v_scaled, PAIRS * b + 2 * g)
                dve.wait_ge(v_proj, PAIRS // 2 * b + g + 1)
                dve.tensor_tensor(vb[:, :, :], p_v[:, :].rearrange("p (t n) -> p t n", t=KT),
                                  bv_bb[:, g * 2 * P:(g + 1) * 2 * P].unsqueeze(1).to_broadcast([P, KT, 2 * P]), ALU.add).then_inc(v_biased, 1)

            def invert_denom(b, p):
                dve.wait_ge(probs_ready, 2 * (PAIRS * b + p) + 2)
                dve.reciprocal(rdenom[:, p % 2], denom[:, p % 2]).then_inc(rdenom_done, 1)

            def scale_values(b, p):
                dve.wait_ge(rdenom_done, PAIRS * b + p + 1)
                dve.wait_ge(v_biased, PAIRS // 2 * b + p // 2 + 1)
                if not (is_int(b) and b == 0 and p < 2):
                    dve.wait_ge(av_done, PAIRS * b + p - 1)
                dve.tensor_tensor(vs[:, p % 2].rearrange("p t (h k) -> p t h k", h=2),
                                  vb[:, :, :].rearrange("p t (h k) -> p t h k", h=4)[:, :, 2 * (p % 2):2 * (p % 2) + 2, :],
                                  rdenom[:, p % 2].unsqueeze(3).to_broadcast([P, KT, 2, DK]), ALU.mult).then_inc(v_scaled, 1)

            def split_xu(u):
                dve.wait_ge(xuT_hi, u.r + 1)
                dve.tensor_tensor(xuT[1][:, u.q, :], p_o[:, L:L + P], xuT[0][:, u.q, :].bitcast(F32), ALU.subtract).then_inc(xuT_lo, 1)

            def unit_product(u, expert):
                at = slice(E * 4 * P, NE * 4 * P) if u.shared else bass.ds(expert * (4 * P), 4 * P)
                if not (is_int(u.n) and u.n == 0):
                    dve.wait_ge(hgl_done, u.n)
                dve.wait_ge(h_done, u.n + 1)
                dve.tensor_tensor(hb[:, :], p_h[:, :], b13[:, at], ALU.add).then_inc(h_biased, 1)
                dve.wait_ge(h_biased, u.n + 1)
                dve.tensor_tensor(hgl[:, u.q, :], hb[:, 2 * P:4 * P], hb[:, 0:2 * P], ALU.mult).then_inc(hgl_done, 1)

            def unit_clip(u):
                dve.wait_ge(hgl_done, u.n + 1)
                dve.tensor_scalar(gmin[:, u.q, :], hgl[:, u.q, 0:P], LIMIT, None, ALU.min).then_inc(g_ready, 1)
                dve.tensor_scalar(lclip[:, u.q, :], hgl[:, u.q, P:2 * P], LIMIT, -LIMIT, ALU.min, ALU.max).then_inc(l_ready, 1)

            def unit_gate(u):
                dve.wait_ge(tanh_done, u.n + 1)
                dve.scalar_tensor_tensor(out=tg[:, u.q, :], in0=th[:, u.q, :], scalar=1.0, in1=gmin[:, u.q, :],
                                         op0=ALU.add, op1=ALU.mult).then_inc(tg_done, 1)

            def unit_linear(u):
                dve.wait_ge(tg_done, u.n + 1)
                if not (is_int(u.n) and u.n < 2):
                    dve.wait_ge(aT_done, u.n - 1)
                dve.scalar_tensor_tensor(out=act_a[:, u.q, :], in0=lclip[:, u.q, :], scalar=1.0, in1=tg[:, u.q, :],
                                         op0=ALU.add, op1=ALU.mult).then_inc(a_ready, 1)

            def finish(b, par):
                dve.wait_ge(wc_done, PAIRS * (b + 1))
                if not (is_int(b) and b < 2):
                    dve.wait_ge(added, 16 * (add_index_of_seq(b - 2) + 1))
                dve.tensor_tensor(yout[par][:, :, :], p_acc[:, 0:L].rearrange("p (t d) -> p t d", t=KT),
                                  out_bias[:, 2, :].unsqueeze(1).to_broadcast([P, KT, P]), ALU.add).then_inc(y_ready, 1)

            def sequence(i, par):
                b = 2 * i + par
                for s in range(STEPS):
                    mask_and_max(b, s)
                    if s == 2 and not (is_int(b) and b == 0):
                        finish(b - 1, 1 - par)
                    if s % 2 == 0:
                        bias_values(b, s // 2)
                    g = stats_at(b, s)
                    if g is not None:
                        ins = statistics(g)
                        if g == GROUPS // 2 - 1:
                            ins.then_inc(rstd_done, 1)
                            add_eps(1)
                    if stats_at(b, s - 1) == GROUPS // 2 - 1:
                        invert_std(1)
                    u = unit(b, s)
                    expert = None
                    if u.routed:
                        if is_int(u.r) and u.r % RT == 0:
                            dve.wait_ge(rt, RT_STEPS * (u.r // RT + 1))
                        if is_int(u.r) and u.r == 0:
                            dve.wait_ge(b13_in[1], 16)
                        expert = dve.value_load(tile_expert[0:1, bass.ds(u.r, 1)], min_val=0, max_val=E - 1)
                    for late, stage in enumerate(routing_stages):
                        h = half_at(b, s, late)
                        if h is not None and stage:
                            stage(h)
                    if w13_at(b, s) is not None:
                        split_w13(w13_at(b, s), p_h)
                    if u.there:
                        unit_product(u, expert)
                    invert_denom(b, s)
                    if u.there:
                        unit_clip(u)
                    scale_values(b, s)
                    if u.there:
                        unit_gate(u)
                    if s + 1 < STEPS and unit(b, s + 1).routed:
                        split_xu(unit(b, s + 1))
                    if u.there:
                        unit_linear(u)
                    g = group_at(b, s, 1)
                    if g is not None:
                        split_xnT(g)

            split_xnT(0)
            dve.wait_ge(xnT_lo, 1)
            for par in range(2):
                dve.tensor_copy(xT[par][:, 1, :], xnT[1][:, 0, par * L:(par + 1) * L].bitcast(F32)).then_inc(first_xT, 1)
            split_w13(E, p_s[0])
            dve.wait_ge(gate_hi, 1)
            dve.tensor_tensor(gateT[1][:, :], p_h[:, P:P + E], gateT[0][:, :].bitcast(F32), ALU.subtract).then_inc(weights_ready, 1)
            dve.wait_ge(small_in, 16 * SMALL)
            dve.tensor_tensor(out_bias[:, 2, :], out_bias[:, 0, :], out_bias[:, 1, :], ALU.add)
            dve.wait_ge(b13_in[0], 16)
            main_loop(dve, sequence)
            finish(B - 1, 1)


_INS = ["source", "Wq", "bq", "Wk", "bk", "Wv", "bv", "Wc", "bc"], ["gate_w", "gate_b", "w1", "b1", "w3", "b3", "w2", "b2",
        "sw1", "sb1", "sw3", "sb3", "sw2", "sb2"]


def kernel(**inputs):
    import numpy as np
    import concourse.bacc as bacc
    from concourse.bass_utils import run_bass_kernel_spmd

    nc = bacc.Bacc("TRN2", target_bir_lowering=False, num_devices=1)
    names = [f"L0_attn_{n}" for n in _INS[0]] + [f"L0_ffn_{n}" for n in _INS[1]]
    arrays = {f"in_{n}": np.ascontiguousarray(inputs[n]) for n in names}
    args = [nc.dram_tensor(n, a.shape, F32, kind="ExternalInput").ap() for n, a in arrays.items()]
    out = nc.dram_tensor("out_0", arrays["in_L0_attn_source"].shape, F32, kind="ExternalOutput").ap()
    build(nc, *args, out)
    return run_bass_kernel_spmd(nc, [arrays], core_ids=[0]).results[0]["out_0"]
```
